# Optimizing a Trainium2 kernel written in Bass

```python
import numpy as np
import jax
import jax.numpy as jnp

def _softmax(x, axis=-1):
    return jax.nn.softmax(x, axis=axis)

def _gelu(x):
    return jax.nn.gelu(x, approximate=True)

def _silu(x):
    return jax.nn.silu(x)

def _sigmoid(x):
    return jax.nn.sigmoid(x)

def _layernorm(x, axis=-1, eps=1e-05):
    m = jnp.mean(x, axis=axis, keepdims=True)
    v = jnp.var(x, axis=axis, keepdims=True)
    return (x - m) / jnp.sqrt(v + eps)

def _scatter_add(tgt, idx, src, axis=0):
    return tgt.at[idx].add(src)

def _segment_sum(src, seg, n):
    return jax.ops.segment_sum(src, seg, n)
kernel_name = 'mk_cond_resid_d2_seqx_r8_35dda5'

def setup_inputs(seed: int=0):
    np.random.seed(seed)
    _w = jnp.asarray

    def _rec_inputs():
        import jax
        import jax.numpy as jnp
        _rk = jax.random.key(seed)
        x = -0.0001538 + 1 * jax.random.normal(jax.random.fold_in(_rk, 1), (128, 32, 128), jnp.float32)
        _lenS = 32 - jax.random.randint(jax.random.fold_in(_rk, 7), (128,), 0, max(1, 32 // 4) + 1, jnp.int32)
        _lenS2 = 32 - jax.random.randint(jax.random.fold_in(_rk, 8), (128,), 0, max(1, 32 // 4) + 1, jnp.int32)
        cond_1024 = 0.00782532 + 1.00527 * jax.random.normal(jax.random.fold_in(_rk, 11), (128, 128), jnp.float32)
        return (x, cond_1024)
    x, cond_1024 = _rec_inputs()

    def _L0_cond_setup():
        import jax, jax.numpy as jnp
        import numpy as np
        NUM_EXPERTS = 4
        TOP_K = 2
        key = jax.random.key(seed)
        ks = jax.random.split(key, 16)
        B, L, D, E, H = (8, 96, 128, NUM_EXPERTS, 512)
        s = 0.02
        return {'context_c': jax.random.normal(ks[0], (B, L, D), jnp.float32), 'time_cond': jax.random.normal(ks[1], (B, D), jnp.float32), 'gate_w': jax.random.normal(ks[2], (3 * D, E), jnp.float32) * s, 'gate_b': jnp.zeros((E,), jnp.float32), 'time_w': jax.random.normal(ks[3], (D, 2 * E), jnp.float32) * s, 'time_b': jnp.zeros((2 * E,), jnp.float32), 'ew1': jax.random.normal(ks[4], (E, D, H), jnp.float32) * s, 'eb1': jnp.zeros((E, H), jnp.float32), 'ew2': jax.random.normal(ks[5], (E, H, D), jnp.float32) * s, 'eb2': jnp.zeros((E, D), jnp.float32), 'sw1': jax.random.normal(ks[6], (D, H), jnp.float32) * s, 'sb1': jnp.zeros((H,), jnp.float32), 'sw2': jax.random.normal(ks[7], (H, D), jnp.float32) * s, 'sb2': jnp.zeros((D,), jnp.float32)}
    _L0_cond_all = _L0_cond_setup()
    _L0_cond_in = {k: v for k, v in _L0_cond_all.items() if k in ('gate_w', 'gate_b', 'time_w', 'time_b', 'ew1', 'eb1', 'ew2', 'eb2', 'sw1', 'sb1', 'sw2', 'sb2')}
    del _L0_cond_all

    def _L1_cond_setup():
        import jax, jax.numpy as jnp
        import numpy as np
        D, HS, HE, E, K = (128, 256, 128, 8, 2)
        B, T = (4, 128)
        N_SHARED = 1
        key = jax.random.key(seed)
        ks = jax.random.split(key, 9)
        g = lambda k, shape, s: jax.random.normal(k, shape, jnp.float32) * s
        return {'x': g(ks[0], (B, T, D), 1.0), 't_emb': g(ks[1], (B, D), 1.0), 'router_W': g(ks[2], (2 * D, E), 0.01), 'router_bias': jnp.zeros((E,), jnp.float32), 'w1': g(ks[3], (D, HS), 0.02), 'w3': g(ks[4], (D, HS), 0.02), 'w2': g(ks[5], (HS, D), 0.02), 'W1e': g(ks[6], (E, D, HE), 0.02), 'W2e': g(ks[7], (E, HE, D), 0.02)}
    _L1_cond_all = _L1_cond_setup()
    _L1_cond_in = {k: v for k, v in _L1_cond_all.items() if k in ('router_W', 'router_bias', 'w1', 'w3', 'w2', 'W1e', 'W2e')}
    del _L1_cond_all
    return {'x': x, 'cond_1024': cond_1024, 'L0_cond_gate_w': _L0_cond_in['gate_w'], 'L0_cond_gate_b': _L0_cond_in['gate_b'], 'L0_cond_time_w': _L0_cond_in['time_w'], 'L0_cond_time_b': _L0_cond_in['time_b'], 'L0_cond_ew1': _L0_cond_in['ew1'], 'L0_cond_eb1': _L0_cond_in['eb1'], 'L0_cond_ew2': _L0_cond_in['ew2'], 'L0_cond_eb2': _L0_cond_in['eb2'], 'L0_cond_sw1': _L0_cond_in['sw1'], 'L0_cond_sb1': _L0_cond_in['sb1'], 'L0_cond_sw2': _L0_cond_in['sw2'], 'L0_cond_sb2': _L0_cond_in['sb2'], 'L1_cond_router_W': _L1_cond_in['router_W'], 'L1_cond_router_bias': _L1_cond_in['router_bias'], 'L1_cond_w1': _L1_cond_in['w1'], 'L1_cond_w3': _L1_cond_in['w3'], 'L1_cond_w2': _L1_cond_in['w2'], 'L1_cond_W1e': _L1_cond_in['W1e'], 'L1_cond_W2e': _L1_cond_in['W2e']}

def reference(x, cond_1024, L0_cond_gate_w, L0_cond_gate_b, L0_cond_time_w, L0_cond_time_b, L0_cond_ew1, L0_cond_eb1, L0_cond_ew2, L0_cond_eb2, L0_cond_sw1, L0_cond_sb1, L0_cond_sw2, L0_cond_sb2, L1_cond_router_W, L1_cond_router_bias, L1_cond_w1, L1_cond_w3, L1_cond_w2, L1_cond_W1e, L1_cond_W2e):
    import jax
    import jax.numpy as jnp

    def _L0_cond_ref(context_c, time_cond, gate_w, gate_b, time_w, time_b, ew1, eb1, ew2, eb2, sw1, sb1, sw2, sb2):
        import jax, jax.numpy as jnp
        import numpy as np
        NUM_EXPERTS = 4
        TOP_K = 2
        B, L, D = context_c.shape
        E, K = (NUM_EXPERTS, TOP_K)
        L_head = L_wrist = L // 3
        head = context_c[:, :L_head]
        wrist = context_c[:, L_head:L_head + L_wrist]
        proprio = context_c[:, L_head + L_wrist:]
        full_agg = context_c.mean(axis=1)
        hp_agg = jnp.concatenate([head, proprio], axis=1).mean(axis=1)
        wp_agg = jnp.concatenate([wrist, proprio], axis=1).mean(axis=1)
        gate_in = jnp.concatenate([full_agg, hp_agg, wp_agg], axis=-1)
        gate_logits = gate_in @ gate_w + gate_b
        mod = jax.nn.silu(time_cond) @ time_w + time_b
        scale, shift = jnp.split(mod, 2, axis=-1)
        gate_logits = gate_logits * (1.0 + scale) + shift
        gate_scores = jax.nn.softmax(gate_logits, axis=-1)
        topk_w, topk_i = jax.lax.top_k(gate_scores, K)
        topk_w = topk_w / (topk_w.sum(axis=-1, keepdims=True) + 1e-08)
        onehot = (topk_i[..., None] == jnp.arange(E)[None, None, :]).astype(context_c.dtype)
        w_be = jnp.sum(topk_w[..., None] * onehot, axis=1)
        mask = np.ones((E, L), dtype=np.float32)
        mask[1, L_head:L_head + L_wrist] = 0.0
        mask[2, :L_head] = 0.0
        mask = jnp.asarray(mask)
        out = jnp.zeros_like(context_c)
        for e in range(E):
            h = jax.nn.gelu(context_c @ ew1[e] + eb1[e], approximate=True)
            y = h @ ew2[e] + eb2[e]
            out = out + w_be[:, e][:, None, None] * mask[e][None, :, None] * y
        shared = jax.nn.gelu(context_c @ sw1 + sb1, approximate=True) @ sw2 + sb2
        return out + shared

    def _L1_cond_ref(x, t_emb, router_W, router_bias, w1, w3, w2, W1e, W2e):
        import jax, jax.numpy as jnp
        import numpy as np
        D, HS, HE, E, K = (128, 256, 128, 8, 2)
        B, T = (4, 128)
        N_SHARED = 1
        Bb, Tt, C = x.shape
        xf = x.reshape(-1, C)
        tf = jnp.broadcast_to(t_emb[:, None, :], (Bb, Tt, C)).reshape(-1, C)
        N = xf.shape[0]
        shared = jax.nn.silu(xf @ w1) * (xf @ w3) @ w2
        s = jax.nn.sigmoid((jnp.concatenate([xf, tf], axis=-1) @ router_W).astype(jnp.float32))
        sel_scores = s + router_bias
        _, topk_idx = jax.lax.top_k(sel_scores, K)
        s_sel = jnp.take_along_axis(s, topk_idx, axis=1)
        denom = s_sel.sum(axis=1, keepdims=True)
        gates = jnp.where(denom > 1e-09, s_sel / (denom + 1e-09), 1.0 / K).astype(x.dtype)
        combine = jnp.zeros((N, E), x.dtype).at[jnp.arange(N)[:, None], topk_idx].add(gates)
        h = jax.nn.gelu(jnp.einsum('nc,ech->enh', xf, W1e), approximate=False)
        y = jnp.einsum('enh,ehc->enc', h, W2e)
        routed = jnp.einsum('ne,enc->nc', combine, y)
        return ((shared + routed) / (N_SHARED + K)).reshape(Bb, Tt, C)
    x = x + _L0_cond_ref(x, cond_1024, L0_cond_gate_w, L0_cond_gate_b, L0_cond_time_w, L0_cond_time_b, L0_cond_ew1, L0_cond_eb1, L0_cond_ew2, L0_cond_eb2, L0_cond_sw1, L0_cond_sb1, L0_cond_sw2, L0_cond_sb2)
    x = x + _L1_cond_ref(x, cond_1024, L1_cond_router_W, L1_cond_router_bias, L1_cond_w1, L1_cond_w3, L1_cond_w2, L1_cond_W1e, L1_cond_W2e)
    return x

_drawn_inputs = setup_inputs


def setup_inputs(seed=0):
    import zlib

    import numpy as np

    out = dict(_drawn_inputs(seed))
    spreads = {'L0_cond_gate_b': (0.0, 0.1),
     'L0_cond_time_b': (0.0, 0.1),
     'L0_cond_eb1': (0.0, 0.498),
     'L0_cond_eb2': (0.0, 0.1),
     'L0_cond_sb1': (0.0, 0.335),
     'L0_cond_sb2': (0.0, 0.1),
     'L1_cond_router_bias': (0.0, 0.8)}
    factors = {'L1_cond_router_W': 8.0,
     'L1_cond_w1': 8.0,
     'L1_cond_w3': 8.0,
     'L1_cond_w2': 8.0,
     'L1_cond_W1e': 8.0,
     'L1_cond_W2e': 8.0}
    for name, (base, spread) in spreads.items():
        noise = np.random.default_rng([zlib.crc32(name.encode()), seed]).standard_normal(out[name].shape)
        drawn = base * np.exp(spread * noise) if base else spread * noise
        out[name] = jnp.asarray(drawn.astype(out[name].dtype))
    for name, factor in factors.items():
        out[name] = (out[name] * factor).astype(out[name].dtype)
    return out
```

```python
from contextlib import ExitStack

import concourse.bass as bass
from concourse import mybir

ALU = mybir.AluOpType
ACT = mybir.ActivationFunctionType
AX = mybir.AxisListType.X
F32 = mybir.dt.float32
F32R = mybir.dt.float32r
BF16 = mybir.dt.bfloat16

P = 128
L = 32
LH = L // 3
LP = L - 2 * LH
E0, H0 = 4, 512
C0 = H0 // P
SH = E0
E1, HS1 = 8, 256
C1 = HS1 // P
TB = 4
BW = TB * P
HW = BW // 2
NB = L // TB
NBM = 2 * LH // TB
NBP = NB - NBM
BIG = 3.0e38

WHOLE = {e: [(e, 0, BW)] for e in (0, 1, 2, 3, SH)}
BOTH = [(1, 0, HW), (2, HW, BW)]
JOBS = {"mixed": [WHOLE[SH], WHOLE[0], BOTH, WHOLE[3]],
        "proprio": [WHOLE[SH], WHOLE[0], WHOLE[1], WHOLE[2], WHOLE[3]]}
L0_PAIRS = 2 * (NBM * 4 + NBP * 5)
L0_PARTS = NBM * 3 + NBP * 4
L1_PAIRS = C1 + E1 // 2
SELECT = 3 * E1

O_W1, O_W3, O_W2 = 0, HS1, 2 * HS1
O_W1E = O_W2 + C1 * P
O_W2E = O_W1E + E1 * P
N_L1W = O_W2E + E1 * P


class Block:

    def __init__(self, kind, start, step=0, first=False):
        self.kind, self.first = kind, first
        self.index = step + start
        if kind == "mixed":
            self.pairs = step * 8 + 8 * start
            self.halves = step * 4 + 4 * start
            self.adds = step * 3 + 3 * start
        elif kind == "proprio":
            past = start - NBM
            self.pairs = step * 10 + (8 * NBM + 10 * past)
            self.halves = step * 5 + (4 * NBM + 5 * past)
            self.adds = step * 4 + (3 * NBM + 4 * past)
        else:
            self.pairs = step * L1_PAIRS + (L0_PAIRS + L1_PAIRS * start)
            self.halves = step * 2 + (L0_PAIRS // 2 + 2 * start)
            self.shared = step * C1 + C1 * start
            self.routed = step * 4 + 4 * start
            self.chunks = step * E1 + E1 * start
        self.at = step * BW + start * BW
        self.columns = slice(self.at, self.at + BW) if isinstance(step, int) else bass.ds(self.at, BW)

    def shifted(self, by):
        at = self.at + by * BW
        return slice(at, at + BW) if isinstance(self.at, int) else bass.ds(at, BW)


def l0_last_adds(kind):
    return len(JOBS[kind]) - 1


def build(nc, x, cond, gate_w, gate_b, time_w, time_b, ew1, eb1, ew2, eb2, sw1, sb1, sw2, sb2,
          router_W, router_bias, w1, w3, w2, W1e, W2e, out):
    ctx = ExitStack()
    with ctx:
        def sb(name, shape, dt=F32):
            return ctx.enter_context(nc.sbuf_tensor("sb_" + name, shape, dt))

        def sem(name):
            return ctx.enter_context(nc.semaphore(name))

        z = ctx.enter_context(nc.psum_tensor("ps_z", [P, 4, BW], F32))
        y = ctx.enter_context(nc.psum_tensor("ps_y", [P, 2, BW], F32))
        m = ctx.enter_context(nc.psum_tensor("ps_m", [P, 2, BW], F32))
        y16, m16 = y[:, :, :].bitcast(BF16), m[:, :, :].bitcast(BF16)

        xnat = sb("xnat", [P, L, P])
        xstage = sb("xstage", [P, TB, P])
        xT = sb("xT", [P, L * P])
        xhi, xlo = sb("xhi", [P, L * P], F32R), sb("xlo", [P, L * P], F32R)
        raw = sb("raw", [P, E0 + 1, 2 * H0])
        whi, wlo = sb("whi", [P, E0 + 1, 2 * H0], F32R), sb("wlo", [P, E0 + 1, 2 * H0], F32R)
        raw1 = raw[:, :, :].rearrange("p e n -> p (e n)")[:, 0:N_L1W]
        vhi, vlo = sb("vhi", [P, N_L1W], F32R), sb("vlo", [P, N_L1W], F32R)
        h = sb("h", [P, 2, 2, BW])
        hhi, hlo = sb("hhi", [P, 2, 2, BW], F32R), sb("hlo", [P, 2, 2, BW], F32R)
        acc = sb("acc", [P, BW])
        part = sb("part", [P, 2, BW])
        ident = sb("ident", [P, P])
        ident16 = sb("ident16", [P, P], BF16)
        ones = sb("ones", [E0, P])
        mask3 = sb("mask3", [E0, 3])
        order = sb("order", [P, E1])
        select = sb("select", [SELECT, E1, P], BF16)
        brow = sb("brow", [21, P])
        bT = sb("bT", [P, 21])
        e2row = sb("e2row", [E0, P])
        vrow = sb("vrow", [1, 20])
        gw = sb("gw", [P, 3, E0])
        tw = sb("tw", [P, 2 * E0])
        rw = sb("rw", [P, 2, E1])
        rhi, rlo = sb("rhi", [P, E1], F32R), sb("rlo", [P, E1], F32R)
        cnat = sb("cnat", [P, P])
        csig = sb("csig", [P, 3, P])
        silu = sb("silu", [P, P])
        cT = sb("cT", [P, 2, P])
        sums = sb("sums", [P, 3, P])
        agg = sb("agg", [P, 3, P])
        aggT = sb("aggT", [P, 3, P])
        rows = sb("rows", [P, 24])
        g0 = sb("g0", [P, 8, E0])
        g0s = sb("g0s", [P, 6])
        wbe = sb("wbe", [P, E0])
        wT = sb("wT", [E0, P])
        wdiag = sb("wdiag", [E0, E0, P])
        wmask = sb("wmask", [E0, 3, P])
        wb = sb("wb", [P, E0, P])
        base = sb("base", [P, 3, P])
        g1 = sb("g1", [P, 5, L, E1])
        g1s = sb("g1s", [P, 6, L])
        gparts = sb("gparts", [P, L, 3, E1], BF16)
        spare = xnat[:, :, :].rearrange("p l d -> p (l d)")
        gT = spare[0:SELECT, 0:L * P // 2].bitcast(BF16)
        x2T = spare[:, L * P // 2:L * P // 2 + BW]
        ostage = spare[:, L * P // 2 + BW:L * P // 2 + 2 * BW].rearrange("p (t d) -> p t d", t=TB)

        x_in, xnat_in, small_in = sem("x_in"), sem("xnat_in"), sem("small_in")
        w_in = [sem(f"w_in{e}") for e in range(E0 + 1)]
        v_in = sem("v_in")
        consts = sem("consts")
        x_turned = sem("x_turned")
        xhi_done, xT_done = sem("xhi_done"), sem("xT_done")
        x_ready = sem("x_ready")
        w_hi_done, w_ready = sem("w_hi_done"), sem("w_ready")
        w_late = sem("w_late")
        v_hi_done, v_ready = sem("v_hi_done"), sem("v_ready")
        r_ready = sem("r_ready")
        z_ready = sem("z_ready")
        h_ready = sem("h_ready")
        hi_act, hi_dve = sem("hi_act"), sem("hi_dve")
        split_done = sem("split_done")
        mm2_done = sem("mm2_done")
        part_ready = sem("part_ready")
        y_used = sem("y_used")
        base_added = sem("base_added")
        adds_done = sem("adds_done")
        x1hi_done, x1_ready = sem("x1hi_done"), sem("x1_ready")
        half_gated, swiglu = sem("half_gated"), sem("swiglu")
        gb_ready = sem("gb_ready")
        gated = sem("gated")
        ghi_done = sem("ghi_done")
        out_turned, stored = sem("out_turned"), sem("stored")
        bank_read = sem("bank_read")
        bT_turned, bT_ready = sem("bT_turned"), sem("bT_ready")
        c_exp, c_turned, rows_mm, rows_ready = sem("c_exp"), sem("c_turned"), sem("rows_mm"), sem("rows_ready")
        c_ready = sem("c_ready")
        silu_ready = sem("silu_ready")
        agg_ready, agg_turned, aggT_ready = sem("agg_ready"), sem("agg_turned"), sem("aggT_ready")
        logits0, shifted0, exp0 = sem("logits0"), sem("shifted0"), sem("exp0")
        wbe_ready, w_turned, wd_ready = sem("wbe_ready"), sem("w_turned"), sem("wd_ready")
        wb_mm, wb_ready = sem("wb_mm"), sem("wb_ready")
        logits1, logits1_ready, exp1 = sem("logits1"), sem("logits1_ready"), sem("exp1")
        gparts_ready, g_turned, gT_ready = sem("gparts_ready"), sem("g_turned"), sem("gT_ready")
        dve_step = sem("dve_step")

        block = ctx.enter_context(nc.Block())

        @block.sync
        def _(sp):
            def two_positions(tensor, at):
                return tensor[:, bass.ds(at, 2), :]

            def load_x(head, second):
                sp.dma_start(xstage[:, 0:2, :], two_positions(x, head)).then_inc(x_in, 16)
                sp.dma_start(xstage[:, 2:4, :], two_positions(x, second)).then_inc(x_in, 16)

            load_x(0, LH)
            sp.dma_start(raw[:, SH, 0:H0], sw1).then_inc(w_in[SH], 16)
            sp.dma_start(raw[:, SH, H0:], sw2.rearrange("(c h) d -> h c d", c=C0)).then_inc(w_in[SH], 16)
            sp.dma_start(raw[:, 0, 0:H0], ew1[0]).then_inc(w_in[0], 16)
            sp.dma_start(raw[:, 0, H0:], ew2[0].rearrange("(c h) d -> h c d", c=C0)).then_inc(w_in[0], 16)
            for n in range(2):
                sp.dma_start(xnat[:, 16 * n:16 * n + 16, :], x[:, 16 * n:16 * n + 16, :]).then_inc(xnat_in, 16)
            sp.wait_ge(x_turned, 1)
            load_x(2, LH + 2)
            for e in range(1, E0):
                sp.dma_start(raw[:, e, 0:H0], ew1[e]).then_inc(w_in[e], 16)
                sp.dma_start(raw[:, e, H0:], ew2[e].rearrange("(c h) d -> h c d", c=C0)).then_inc(w_in[e], 16)
            with sp.Fori(0, NBM - 2) as r:
                sp.wait_ge(x_turned, r + 2)
                load_x(r * 2 + 4, r * 2 + (LH + 4))
            with sp.Fori(0, NBP) as r:
                sp.wait_ge(x_turned, r + NBM)
                load_x(r * 4 + 2 * LH, r * 4 + (2 * LH + 2))
            sp.wait_ge(w_ready, 2)
            sp.wait_ge(w_late, E0 - 1)
            for at, n, src in ((O_W1, HS1, w1), (O_W3, HS1, w3),
                               (O_W2, C1 * P, w2.rearrange("(c h) d -> h c d", c=C1)),
                               (O_W1E, E1 * P, W1e.rearrange("e c h -> c e h")),
                               (O_W2E, E1 * P, W2e.rearrange("e h d -> h e d"))):
                sp.dma_start(raw1[:, at:at + n], src).then_inc(v_in, 16)

            def store(first, second, copied):
                sp.wait_ge(bank_read, copied + 1)
                sp.dma_start(two_positions(out, first), ostage[:, 0:2, :]).then_inc(stored, 16)
                sp.dma_start(two_positions(out, second), ostage[:, 2:4, :]).then_inc(stored, 16)

            with sp.Fori(0, NBM) as r:
                store(r * 2, r * 2 + LH, r + 1)
            with sp.Fori(0, NBP) as r:
                store(r * 4 + 2 * LH, r * 4 + (2 * LH + 2), r + (NBM + 1))
            sp.wait_ge(stored, 32 * NB)

        @block.gpsimd
        def _(pool):
            pool.memset(ident[:, :], 0.0).then_inc(consts, 1)
            pool.memset(ident16[:, :], 0.0).then_inc(consts, 1)
            pool.memset(select[:, :, :], 0.0).then_inc(consts, 1)
            pool.memset(mask3[:, :], 1.0).then_inc(consts, 1)
            pool.memset(ones[:, :], 1.0).then_inc(consts, 1)
            pool.wait_ge(consts, 5)
            for tile in (ident, ident16):
                pool.affine_select(out=tile[:, :], in_=tile[:, :], compare_op=ALU.not_equal, fill=1.0,
                                   base=0, pattern=[[-1, P]], channel_multiplier=1).then_inc(consts, 1)
            pool.affine_select(out=mask3[:, 0:2], in_=mask3[:, 0:2], compare_op=ALU.not_equal, fill=0.0,
                               base=-2, pattern=[[1, 2]], channel_multiplier=1).then_inc(consts, 1)
            for k in range(3):
                pool.wait_ge(consts, 8 + k)
                pool.affine_select(out=select[:, :, :], in_=select[:, :, :], compare_op=ALU.not_equal,
                                   fill=1.0, base=-E1 * k, pattern=[[-1, E1], [0, P]],
                                   channel_multiplier=1).then_inc(consts, 1)
            for e in range(E1):
                pool.memset(order[:, e:e + 1], float(E1 - e)).then_inc(consts, 1)

            def x_lo(b, columns, number):
                pool.wait_ge(xhi_done, number)
                pool.tensor_tensor(xlo[:, columns], xT[:, columns], xhi[:, columns].bitcast(F32),
                                   ALU.subtract).then_inc(x_ready, 1)

            def w_lo(e):
                pool.wait_ge(w_hi_done, e)
                pool.tensor_tensor(wlo[:, e, :], raw[:, e, :], whi[:, e, :].bitcast(F32),
                                   ALU.subtract).then_inc(w_late, 1)

            def add_base(b):
                pool.wait_ge(y_used, b.index + 1)
                pool.wait_ge(wb_ready, 2)
                if b.kind == "mixed":
                    other = base[:, 0:2, :].unsqueeze(2).to_broadcast([P, 2, 2, P])
                    own = acc[:, :].rearrange("p (a b c) -> p a b c", a=2, b=2)
                else:
                    other = base[:, 2, :].unsqueeze(1).to_broadcast([P, TB, P])
                    own = acc[:, :].rearrange("p (b c) -> p b c", b=TB)
                pool.tensor_tensor(own, own, other, ALU.add).then_inc(base_added, 1)

            def add_parts(b):
                for j in range(1, len(JOBS[b.kind])):
                    pool.wait_ge(part_ready, b.adds + j)
                    if j == 1:
                        pool.wait_ge(base_added, b.index + 1)
                    else:
                        pool.wait_ge(adds_done, b.adds + (j - 1))
                    pool.tensor_tensor(acc[:, :], acc[:, :], part[:, j % 2, :], ALU.add).then_inc(adds_done, 1)

            def l0_block(b, next_x):
                if next_x:
                    x_lo(b, b.shifted(1), b.index + 2)
                add_base(b)
                add_parts(b)

            x_lo(None, slice(0, BW), 1)
            for e in range(1, E0):
                w_lo(e)
            l0_block(Block("mixed", 0, first=True), True)
            with pool.Fori(0, NBM - 1) as r:
                l0_block(Block("mixed", 1, r), True)
            with pool.Fori(0, NBP - 1) as r:
                l0_block(Block("proprio", NBM, r), True)
            for n, (at, end) in enumerate(((0, O_W1E), (O_W1E, O_W2E), (O_W2E, N_L1W))):
                pool.wait_ge(v_hi_done, n + 1)
                pool.tensor_tensor(vlo[:, at:end], raw1[:, at:end], vhi[:, at:end].bitcast(F32),
                                   ALU.subtract).then_inc(v_ready, 1)
            l0_block(Block("proprio", NB - 1), False)

        @block.scalar
        def _(act):
            act.dma_start(brow[0:16, :], eb1.rearrange("e (c h) -> (e c) h", c=C0)).then_inc(small_in, 16)
            act.dma_start(brow[16:20, :], sb1.rearrange("(c h) -> c h", c=C0)).then_inc(small_in, 16)
            act.dma_start(brow[20:21, :], sb2.rearrange("(a h) -> a h", a=1)).then_inc(small_in, 16)
            act.dma_start(cnat[:, :], cond).then_inc(small_in, 16)
            act.dma_start(e2row[:, :], eb2).then_inc(small_in, 16)
            act.dma_start(vrow[:, 0:4], gate_b.rearrange("(a h) -> a h", a=1)).then_inc(small_in, 16)
            act.dma_start(vrow[:, 4:12], time_b.rearrange("(a h) -> a h", a=1)).then_inc(small_in, 16)
            act.dma_start(vrow[:, 12:20], router_bias.rearrange("(a h) -> a h", a=1)).then_inc(small_in, 16)
            act.dma_start(gw[:, :, :], gate_w.rearrange("(j p) e -> p j e", j=3)).then_inc(small_in, 16)
            act.dma_start(tw[:, :], time_w).then_inc(small_in, 16)
            act.dma_start(rw[:, :, :], router_W.rearrange("(j p) e -> p j e", j=2)).then_inc(small_in, 16)

            def x_hi(columns, number):
                act.wait_ge(xT_done, number)
                act.activation(xhi[:, columns], xT[:, columns], ACT.Copy).then_inc(xhi_done, 1)

            def w_hi(e):
                act.wait_ge(w_in[e], 32)
                act.activation(whi[:, e, :], raw[:, e, :], ACT.Copy).then_inc(w_hi_done, 1)

            def hidden_l0(b, p):
                buf = p % 2
                for j in range(2):
                    c = 2 * (p % 2) + j
                    act.wait_ge(z_ready, b.pairs * 2 + (2 * p + j + 1))
                    if j == 0 and not (b.first and p < 2):
                        act.wait_ge(split_done, b.pairs + (p - 1))
                    for e, lo, hi in JOBS[b.kind][p // 2]:
                        last = act.activation(h[:, buf, j, lo:hi], z[:, 2 * buf + j, lo:hi],
                                              ACT.Gelu_apprx_tanh, bias=bT[:, C0 * e + c:C0 * e + c + 1])
                last.then_inc(h_ready, 1)
                if p % 2 == 0:
                    act.wait_ge(h_ready, b.pairs + (p + 1))
                    if not (b.first and p < 2):
                        act.wait_ge(mm2_done, b.pairs + (p - 1))
                    act.activation(hhi[:, buf, :, :], h[:, buf, :, :], ACT.Copy).then_inc(hi_act, 1)

            def l0_block(b, next_x, hooks=None):
                for p in range(2 * len(JOBS[b.kind])):
                    hidden_l0(b, p)
                    if p == 2 and next_x:
                        x_hi(b.shifted(1), b.index + 2)
                    if hooks:
                        hooks(p)

            def first_hooks(p):
                if 0 <= p < 3:
                    w_hi(p + 1)
                if p == 3:
                    act.wait_ge(shifted0, 2)
                    act.activation(g0[:, 2, :], g0[:, 1, :], ACT.Exp, bias=g0s[:, 0:1],
                                   accum_out=g0s[:, 1:2]).then_inc(exp0, 1)

            def last_hooks(p):
                if p < 3:
                    at, end = ((0, O_W1E), (O_W1E, O_W2E), (O_W2E, N_L1W))[p]
                    act.wait_ge(v_in, 16 * 5)
                    act.activation(vhi[:, at:end], raw1[:, at:end], ACT.Copy).then_inc(v_hi_done, 1)
                if p == 4:
                    exp_router(0, L - TB, 1)
                if p == 9:
                    turned_gates(0, m16[0:SELECT, 0, :])
                    turned_gates(1, m16[0:SELECT, 1, :])

            def exp_router(t0, t1, number):
                act.wait_ge(logits1_ready, number)
                act.activation(g1[:, 1, t0:t1, :], g1[:, 0, t0:t1, :], ACT.Exp, scale=-1.0).then_inc(exp1, 1)

            def gated_hi(b, p, before):
                for j in range(2):
                    n = b.chunks + (2 * (p - 2) + j + 1 - (E1 if before else 0))
                    act.wait_ge(gated, n)
                    if j == 0:
                        act.wait_ge(mm2_done, b.pairs + (p - 1 - (L1_PAIRS if before else 0)))
                    act.activation(hhi[:, p % 2, j, :], h[:, p % 2, j, :], ACT.Copy).then_inc(ghi_done, 1)

            def copy_out(number):
                act.wait_ge(out_turned, number)
                if not (isinstance(number, int) and number == 1):
                    act.wait_ge(stored, (number - 1) * 32)
                act.activation(ostage, y[:, 1, :].rearrange("p (t d) -> p t d", t=TB),
                               ACT.Copy).then_inc(bank_read, 1)

            def l1_block(b, hooks=None):
                for p in range(L1_PAIRS):
                    buf = p % 2
                    if p == 0 and not b.first:
                        gated_hi(b, L1_PAIRS - 1, True)
                    if p > 2:
                        gated_hi(b, p - 1, False)
                    act.wait_ge(split_done, b.pairs + (p - 1))
                    if p < C1:
                        act.wait_ge(z_ready, b.pairs * 2 + (2 * p + 1))
                        act.activation(h[:, buf, 0, :], z[:, 2 * buf, :], ACT.Tanh, scale=0.5).then_inc(h_ready, 1)
                    else:
                        act.wait_ge(z_ready, b.pairs * 2 + (2 * p + 2))
                        act.activation(h[:, buf, :, :], z[:, 2 * buf:2 * buf + 2, :], ACT.Gelu).then_inc(h_ready, 1)
                    if p == 2 and not b.first:
                        copy_out(b.index)
                    if hooks:
                        hooks(p)

            def turned_gates(fill, src):
                act.wait_ge(g_turned, fill + 1)
                act.activation(gT[:, fill * 8 * P:(fill + 1) * 8 * P], src,
                               ACT.Copy).then_inc(bank_read if fill == L // 8 - 1 else gT_ready, 1)

            act.wait_ge(small_in, 16 * 11)
            act.activation(csig[:, 0, :], cnat[:, :], ACT.Exp, scale=-1.0).then_inc(c_exp, 1)
            x_hi(slice(0, BW), 1)
            act.wait_ge(bT_ready, 1)
            l0_block(Block("mixed", 0, first=True), True, first_hooks)
            with act.Fori(0, NBM - 1) as r:
                l0_block(Block("mixed", 1, r), True)
            with act.Fori(0, NBP - 1) as r:
                l0_block(Block("proprio", NBM, r), True)
            l0_block(Block("proprio", NB - 1), False, last_hooks)

            def first_l1_hooks(p):
                if p == 1:
                    turned_gates(2, y16[0:SELECT, 1, :])
                if p == 4:
                    exp_router(L - TB, L, 2)

            l1_block(Block("l1", 0, first=True), first_l1_hooks)

            def second_l1_hooks(p):
                if p == 0:
                    turned_gates(3, y16[0:SELECT, 1, :])

            l1_block(Block("l1", 1), second_l1_hooks)
            with act.Fori(0, NB - 3) as r:
                l1_block(Block("l1", 2, r))
            l1_block(Block("l1", NB - 1))
            gated_hi(Block("l1", NB), L1_PAIRS - 1, True)
            copy_out(NB)

        @block.tensor
        def _(pe):
            def three(dst, hi, lo, rhs_hi, rhs_lo, start, stop, **kw):
                pe.matmul(dst, hi, rhs_hi, start=start, stop=False, **kw)
                pe.matmul(dst, lo, rhs_hi, start=False, stop=False, **kw)
                return pe.matmul(dst, hi, rhs_lo, start=False, stop=stop, **kw)

            def turn_x(number):
                pe.wait_ge(x_in, number * 32)
                if not (isinstance(number, int) and number == 1):
                    pe.wait_ge(xT_done, number - 1)
                for t in range(TB):
                    last = pe.transpose(m[:, 0, t * P:(t + 1) * P], xstage[:, t, :], ident[:, :])
                last.then_inc(x_turned, 1)

            def first_layer_l0(b, p, by=0):
                buf = p % 2
                if not (b.first and p < 2 and not by):
                    pe.wait_ge(h_ready, b.pairs + (p - 1))
                if p == 0:
                    pe.wait_ge(x_ready, b.index + 1)
                for j in range(2):
                    c = 2 * (p % 2) + j
                    for e, lo, hi in JOBS[b.kind][p // 2]:
                        cols = bass.ds(b.at + lo, hi - lo)
                        last = three(z[:, 2 * buf + j, lo:hi], whi[:, e, c * P:(c + 1) * P],
                                     wlo[:, e, c * P:(c + 1) * P], xhi[:, cols], xlo[:, cols], True, True)
                    last.then_inc(z_ready, 1)

            def second_layer_l0(b, p):
                n_jobs = len(JOBS[b.kind])
                j0, buf = p // 2, p % 2
                bank = (n_jobs - 1 - j0) % 2
                pe.wait_ge(split_done, b.pairs + (p + 1))
                if p % 2 == 0:
                    if j0 == 2:
                        pe.wait_ge(y_used, b.index + 1)
                    elif j0 > 2:
                        pe.wait_ge(part_ready, b.adds + (j0 - 2))
                    elif not b.first:
                        pe.wait_ge(part_ready, b.adds)
                segments = JOBS[b.kind][j0]
                for j in range(2):
                    c = 2 * (p % 2) + j
                    for n, (e, lo, hi) in enumerate(segments):
                        at = H0 + c * P
                        last = three(y[:, bank, lo:hi], whi[:, e, at:at + P], wlo[:, e, at:at + P],
                                     hhi[:, buf, j, lo:hi], hlo[:, buf, j, lo:hi],
                                     c == 0 and n == 0, c == C0 - 1, skip_group_check=len(segments) > 1)
                last.then_inc(mm2_done, 1)

            def l0_block(b, following, next_x, hooks=None):
                n = 2 * len(JOBS[b.kind])
                for p in range(n):
                    if b.first and p == 0:
                        pe.wait_ge(w_ready, 2)
                    if b.first and p in (2, 4):
                        pe.wait_ge(w_late, 2 if p == 2 else 3)
                    if p + 2 < n:
                        first_layer_l0(b, p + 2)
                    else:
                        following(p + 2 - n)
                    second_layer_l0(b, p)
                    if p == 1 and next_x:
                        turn_x(b.index + 2)
                    if hooks:
                        hooks(p)

            def first_hooks(p):
                if p == 0:
                    pe.wait_ge(silu_ready, 1)
                    pe.transpose(m[:, 1, 0:P], silu[:, :], ident[:, :])
                    pe.transpose(m[:, 1, P:2 * P], cnat[:, :], ident[:, :]).then_inc(c_turned, 1)
                if p == 1:
                    pe.wait_ge(c_ready, 1)
                    pe.matmul(m[:, 1, 384:392], cT[:, 0, :], tw[:, :], start=True, stop=False)
                    pe.matmul(m[:, 1, 384:392], ones[0:1, :], vrow[:, 4:12], start=False, stop=True)
                    pe.matmul(m[:, 1, 392:400], cT[:, 1, :], rw[:, 1, :], start=True, stop=True)
                    pe.matmul(m[:, 1, 400:408], ones[0:1, :], vrow[:, 12:20], start=True, stop=True).then_inc(rows_mm, 1)
                if p == 4:
                    pe.wait_ge(wb_ready, 2)
                if p == 3:
                    pe.wait_ge(rows_ready, 1)
                    pe.wait_ge(agg_ready, 1)
                    for j in range(3):
                        last = pe.transpose(m[:, 1, j * P:(j + 1) * P], agg[:, j, :], ident[:, :])
                    last.then_inc(agg_turned, 1)
                    pe.wait_ge(aggT_ready, 2)
                    for j in range(3):
                        pe.matmul(m[:, 1, 408:412], aggT[:, j, :], gw[:, j, :], start=j == 0, stop=False)
                    pe.matmul(m[:, 1, 408:412], ones[0:1, :], vrow[:, 0:4], start=False, stop=True).then_inc(logits0, 1)
                    pe.wait_ge(wbe_ready, 1)
                    pe.matmul(m[0:E0, 1, 0:P], wbe[:, :], ident[:, :], start=True, stop=True).then_inc(w_turned, 1)
                    pe.wait_ge(wd_ready, 2)
                    pe.wait_ge(x_ready, 2)
                    pe.matmul(m[:, 1, :], ones[:, :], wdiag[:, :, :].rearrange("k e b -> k (e b)"),
                              start=True, stop=True).then_inc(wb_mm, 1)
                    pe.matmul(m[:, 0, 0:3 * P], e2row[:, :], wmask[:, :, :].rearrange("k e b -> k (e b)"),
                              start=True, stop=True).then_inc(wb_mm, 1)

            def route(t0, t1, dst):
                for t in range(t0, t1):
                    at = slice(t * P, (t + 1) * P)
                    last = three(dst[:, (t - t0) * E1:(t - t0 + 1) * E1], xhi[:, at], xlo[:, at],
                                 rhi[:, :], rlo[:, :], True, True)
                last.then_inc(logits1, 1)

            def turn_gates(fill, dst):
                for t in range(8):
                    last = pe.transpose(dst[:, t * P:(t + 1) * P],
                                        gparts[:, fill * 8 + t, :, :].rearrange("p k e -> p (k e)"), ident16[:, :])
                last.then_inc(g_turned, 1)

            def last_hooks(p):
                if p == 2:
                    pe.wait_ge(x1_ready, 2 * (NB - 1))
                    pe.wait_ge(r_ready, 2)
                    route(0, L - TB, m[:, 1, :])
                if p == 8:
                    pe.wait_ge(gparts_ready, 1)
                    pe.wait_ge(logits1_ready, 1)
                    turn_gates(0, m16[0:SELECT, 0, :])
                    turn_gates(1, m16[0:SELECT, 1, :])

            def first_layer_l1(b, p, gates=None):
                buf = p % 2
                if p in (2, 3):
                    pe.wait_ge(swiglu, b.shared + (p - 1))
                else:
                    pe.wait_ge(h_ready, b.pairs + (p - 1))
                if gates and not (gates[0].first and gates[1] == 2):
                    pe.wait_ge(gated, gates[0].chunks + 2 * (gates[1] - 2))
                if p < 2:
                    offsets = (O_W1 + p * P, O_W3 + p * P)
                else:
                    offsets = tuple(O_W1E + (2 * (p - 2) + j) * P for j in range(2))
                for j, at in enumerate(offsets):
                    three(z[:, 2 * buf + j, :], vhi[:, at:at + P], vlo[:, at:at + P],
                          xhi[:, b.columns], xlo[:, b.columns], True, True).then_inc(z_ready, 1)
                    if gates and j == 0:
                        gates_out(*gates)

            def gates_out(b, p):
                for j in range(2):
                    last = pe.matmul(m[:, j, :], select[:, 2 * (p - 2) + j, :], gT[:, b.columns],
                                     start=True, stop=True)
                last.then_inc(gb_ready, 1)

            def second_layer_l1(b, p):
                buf = p % 2
                if p == 0 and b.first:
                    pe.wait_ge(part_ready, L0_PARTS)
                elif p == 0:
                    pe.wait_ge(y_used, b.index + NB)
                pe.wait_ge(split_done, b.pairs + (p + 1))
                if p < 2:
                    at = O_W2 + p * P
                    last = three(y[:, 0, :], vhi[:, at:at + P], vlo[:, at:at + P],
                                 hhi[:, buf, 0, :], hlo[:, buf, 0, :], p == 0, False)
                else:
                    for j in range(2):
                        at = O_W2E + (2 * (p - 2) + j) * P
                        last = three(y[:, 0, :], vhi[:, at:at + P], vlo[:, at:at + P],
                                     hhi[:, buf, j, :], hlo[:, buf, j, :], False, p == L1_PAIRS - 1 and j == 1)
                last.then_inc(mm2_done, 1)

            def turn_out(number):
                pe.wait_ge(y_used, number + NB)
                pe.wait_ge(bank_read, number)
                for t in range(TB):
                    last = pe.transpose(y[:, 1, t * P:(t + 1) * P], x2T[:, t * P:(t + 1) * P], ident[:, :])
                last.then_inc(out_turned, 1)

            def l1_block(b, following=None, hooks=None):
                for p in range(L1_PAIRS):
                    if b.first and p == 1:
                        pe.wait_ge(gT_ready, 3)
                    gates = (b, p + 1) if 2 <= p + 1 < L1_PAIRS else None
                    if p + 2 < L1_PAIRS:
                        first_layer_l1(b, p + 2, gates)
                    elif following:
                        following(p + 2 - L1_PAIRS, gates)
                    elif gates:
                        pe.wait_ge(gated, b.chunks + 2 * (p - 1))
                        gates_out(*gates)
                    second_layer_l1(b, p)
                    if p == 1 and not b.first:
                        turn_out(b.index)
                    if hooks:
                        hooks(p)

            pe.wait_ge(consts, 8)
            pe.wait_ge(small_in, 16 * 11)
            turn_x(1)
            pe.transpose(y[:, 0, 0:21], brow[:, :], ident[0:21, 0:21]).then_inc(bT_turned, 1)
            b = Block("mixed", 0, first=True)
            pe.wait_ge(w_ready, 1)
            first_layer_l0(b, 0)
            first_layer_l0(b, 1)
            pe.wait_ge(bT_ready, 1)
            l0_block(b, lambda p: first_layer_l0(Block("mixed", 1), p), True, first_hooks)
            with pe.Fori(0, NBM - 1) as r:
                l0_block(Block("mixed", 1, r), lambda p: first_layer_l0(Block("mixed", 2, r), p), True)
            with pe.Fori(0, NBP - 1) as r:
                l0_block(Block("proprio", NBM, r), lambda p: first_layer_l0(Block("proprio", NBM + 1, r), p), True)

            def into_l1(p):
                if p == 0:
                    pe.wait_ge(consts, 19)
                    pe.wait_ge(v_ready, 3)
                first_layer_l1(Block("l1", 0, first=True), p)

            l0_block(Block("proprio", NB - 1), into_l1, False, last_hooks)

            def first_l1_hooks(p):
                if p == 0:
                    pe.wait_ge(part_ready, L0_PARTS)
                    turn_gates(2, y16[0:SELECT, 1, :])
                if p == 2:
                    pe.wait_ge(x1_ready, 2 * NB)
                    route(L - TB, L, y[:, 1, :])
                if p == 5:
                    pe.wait_ge(gparts_ready, 2)
                    turn_gates(3, y16[0:SELECT, 1, :])

            l1_block(Block("l1", 0, first=True), lambda p, g: first_layer_l1(Block("l1", 1), p, g), first_l1_hooks)
            with pe.Fori(0, NB - 2) as r:
                l1_block(Block("l1", 1, r), lambda p, g: first_layer_l1(Block("l1", 2, r), p, g))
            l1_block(Block("l1", NB - 1))
            turn_out(NB)

        @block.vector
        def _(dve):
            steps = [0]

            def link(ins):
                steps[0] += 1
                ins.then_inc(dve_step, 1)
                dve.wait_ge(dve_step, steps[0])

            def tt(out_, a, b_, op):
                return dve.tensor_tensor(out_, a, b_, op)

            def x_copy(columns, number):
                dve.wait_ge(x_turned, number)
                dve.tensor_copy(xT[:, columns], m[:, 0, :]).then_inc(xT_done, 1)

            def split_l0(b, p):
                buf = p % 2
                if p % 2 == 0:
                    dve.wait_ge(hi_act, b.halves + (p // 2 + 1))
                else:
                    dve.wait_ge(h_ready, b.pairs + (p + 1))
                    if not (b.first and p < 2):
                        dve.wait_ge(mm2_done, b.pairs + (p - 1))
                    dve.tensor_copy(hhi[:, buf, :, :], h[:, buf, :, :]).then_inc(hi_dve, 1)
                    dve.wait_ge(hi_dve, b.halves + (p // 2 + 1))
                tt(hlo[:, buf, :, :], h[:, buf, :, :], hhi[:, buf, :, :].bitcast(F32),
                   ALU.subtract).then_inc(split_done, 1)

            def job_out(b, j, columns, before=None):
                n_jobs = len(JOBS[b.kind])
                bank = (n_jobs - 1 - j) % 2
                dve.wait_ge(mm2_done, b.pairs + (2 * j + 2))
                if j == 0:
                    if not b.first:
                        dve.wait_ge(x1_ready, b.index * 2)
                    tt(acc[:, :], y[:, bank, :], xT[:, columns], ALU.add).then_inc(y_used, 1)
                    return
                if j >= 3:
                    dve.wait_ge(adds_done, b.adds + (j - 2))
                if JOBS[b.kind][j] is BOTH:
                    weights = wb[:, 1:3, :].unsqueeze(2).to_broadcast([P, 2, 2, P])
                    shape = dict(a=2, b=2)
                    src = y[:, bank, :].rearrange("p (a b c) -> p a b c", **shape)
                    dst = part[:, j % 2, :].rearrange("p (a b c) -> p a b c", **shape)
                else:
                    e = JOBS[b.kind][j][0][0]
                    weights = wb[:, e, :].unsqueeze(1).to_broadcast([P, TB, P])
                    src = y[:, bank, :].rearrange("p (b c) -> p b c", b=TB)
                    dst = part[:, j % 2, :].rearrange("p (b c) -> p b c", b=TB)
                tt(dst, src, weights, ALU.mult).then_inc(part_ready, 1)

            def close_l0(b):
                dve.wait_ge(adds_done, b.adds + l0_last_adds(b.kind))
                dve.tensor_copy(xhi[:, b.columns], acc[:, :]).then_inc(x1hi_done, 1)
                dve.tensor_copy(xT[:, b.columns], acc[:, :]).then_inc(x1_ready, 1)
                dve.wait_ge(x1hi_done, b.index + 1)
                tt(xlo[:, b.columns], acc[:, :], xhi[:, b.columns].bitcast(F32),
                   ALU.subtract).then_inc(x1_ready, 1)

            def l0_block(b, before, next_x, hooks=None):
                n_jobs = len(JOBS[b.kind])
                for p in range(2 * n_jobs):
                    split_l0(b, p)
                    if p == 2 and next_x:
                        x_copy(b.shifted(1), b.index + 2)
                    if before is not None and p == 0:
                        job_out(before, len(JOBS[before.kind]) - 1, before.columns)
                    if before is not None and p == 1:
                        close_l0(before)
                    if hooks:
                        hooks(p)
                    if p >= 2 and p % 2 == 0:
                        job_out(b, p // 2 - 1, b.columns)

            def wide(v, t, n):
                return v.unsqueeze(2).to_broadcast([P, t, n])

            def pick(values, best, scratch, chosen, t, n):
                ranks = order[:, E1 - n:].unsqueeze(1).to_broadcast([P, t, n])
                link(dve.tensor_reduce(best, values, AX, ALU.max))
                link(tt(scratch, values, wide(best, t, n), ALU.is_equal))
                link(tt(scratch, scratch, ranks, ALU.mult))
                link(dve.tensor_reduce(best, scratch, AX, ALU.max))
                link(tt(chosen, scratch, wide(best, t, n), ALU.is_equal))

            def without(values, chosen, rest):
                link(dve.scalar_tensor_tensor(out=rest, in0=chosen, scalar=-BIG, in1=values,
                                              op0=ALU.mult, op1=ALU.add))

            def cond_prepare():
                dve.wait_ge(c_exp, 1)
                link(dve.tensor_scalar(csig[:, 1, :], csig[:, 0, :], 1.0, None, ALU.add))
                link(dve.reciprocal(csig[:, 2, :], csig[:, 1, :]))
                tt(silu[:, :], cnat[:, :], csig[:, 2, :], ALU.mult).then_inc(silu_ready, 1)

            def positions_sum(k, l0, l1):
                return dve.tensor_reduce(sums[:, k, :], xnat[:, l0:l1, :].rearrange("p l d -> p d l"), AX, ALU.add)

            def gate_l0():
                dve.wait_ge(rows_mm, 1)
                dve.tensor_copy(rows[:, :], m[:, 1, 384:408]).then_inc(rows_ready, 1)
                link(tt(agg[:, 1, :], sums[:, 0, :], sums[:, 2, :], ALU.add))
                link(tt(agg[:, 0, :], agg[:, 1, :], sums[:, 1, :], ALU.add))
                tt(agg[:, 2, :], sums[:, 1, :], sums[:, 2, :], ALU.add).then_inc(agg_ready, 1)
                dve.wait_ge(agg_turned, 1)
                dve.tensor_scalar(aggT[:, 0, :], m[:, 1, 0:P], 1.0 / L, None, ALU.mult).then_inc(aggT_ready, 1)
                dve.tensor_scalar(aggT[:, 1:3, :], m[:, 1, P:3 * P].rearrange("p (a d) -> p a d", a=2),
                                  1.0 / (LH + LP), None, ALU.mult).then_inc(aggT_ready, 1)
                dve.wait_ge(rows_ready, 1)
                dve.wait_ge(logits0, 1)
                link(dve.scalar_tensor_tensor(out=g0[:, 0, :], in0=rows[:, 0:E0], scalar=1.0, in1=m[:, 1, 408:412],
                                              op0=ALU.add, op1=ALU.mult))
                tt(g0[:, 1, :], g0[:, 0, :], rows[:, E0:2 * E0], ALU.add).then_inc(shifted0, 1)
                dve.wait_ge(shifted0, 1)
                dve.tensor_reduce(g0s[:, 0:1], g0[:, 1, :], AX, ALU.max, negate=True).then_inc(shifted0, 1)
                dve.wait_ge(exp0, 1)
                link(dve.reciprocal(g0s[:, 2:3], g0s[:, 1:2]))
                link(dve.tensor_scalar(g0[:, 3, :], g0[:, 2, :], g0s[:, 2:3], None, ALU.mult))
                one = slice(3, 4)
                pick(g0[:, 3:4, :], g0s[:, one], g0[:, 4:5, :], g0[:, 5:6, :], 1, E0)
                without(g0[:, 3, :], g0[:, 5, :], g0[:, 6, :])
                pick(g0[:, 6:7, :], g0s[:, one], g0[:, 4:5, :], g0[:, 7:8, :], 1, E0)
                link(tt(g0[:, 4, :], g0[:, 5, :], g0[:, 7, :], ALU.add))
                link(tt(g0[:, 5, :], g0[:, 4, :], g0[:, 3, :], ALU.mult))
                link(dve.tensor_reduce(g0s[:, 4:5], g0[:, 5, :], AX, ALU.add))
                link(dve.tensor_scalar(g0s[:, 5:6], g0s[:, 4:5], 1e-8, None, ALU.add))
                link(dve.reciprocal(g0s[:, 4:5], g0s[:, 5:6]))
                dve.tensor_scalar(wbe[:, :], g0[:, 5, :], g0s[:, 4:5], None, ALU.mult).then_inc(wbe_ready, 1)
                dve.wait_ge(w_turned, 1)
                link(dve.tensor_copy(wT[:, :], m[0:E0, 1, 0:P]))
                tt(wdiag[:, :, :], wT[:, :].unsqueeze(1).to_broadcast([E0, E0, P]),
                   ident[0:E0, 0:E0].unsqueeze(2).to_broadcast([E0, E0, P]), ALU.mult).then_inc(wd_ready, 1)
                tt(wmask[:, :, :], wT[:, :].unsqueeze(1).to_broadcast([E0, 3, P]),
                   mask3[:, :].unsqueeze(2).to_broadcast([E0, 3, P]), ALU.mult).then_inc(wd_ready, 1)
                dve.wait_ge(wb_mm, 2)
                dve.tensor_copy(wb[:, :, :], m[:, 1, :].rearrange("p (e b) -> p e b", e=E0)).then_inc(wb_ready, 1)
                dve.tensor_scalar(base[:, :, :], m[:, 0, 0:3 * P].rearrange("p (k b) -> p k b", k=3),
                                  bT[:, 20:21], None, ALU.add).then_inc(wb_ready, 1)
                dve.wait_ge(wb_ready, 1)

            def first_hooks(p):
                if p == 0:
                    dve.wait_ge(xnat_in, 32)
                    positions_sum(0, 0, LH)
                    dve.wait_ge(c_turned, 1)
                    dve.tensor_copy(cT[:, :, :], m[:, 1, 0:2 * P].rearrange("p (a d) -> p a d", a=2)).then_inc(c_ready, 1)
                if p == 1:
                    positions_sum(1, LH, 2 * LH)
                if p == 2:
                    link(positions_sum(2, 2 * LH, L))
                if p == 3:
                    gate_l0()

            def logits_l1(t0, t1, src, number):
                dve.wait_ge(logits1, number)
                t = t1 - t0
                tt(g1[:, 0, t0:t1, :], src[:, 0:t * E1].rearrange("p (t e) -> p t e", e=E1),
                   rows[:, 8:16].unsqueeze(1).to_broadcast([P, t, E1]), ALU.add).then_inc(logits1_ready, 1)

            def scores_l1(t0, t1, number):
                t = t1 - t0
                dve.wait_ge(exp1, number)
                link(dve.tensor_scalar(g1[:, 2, t0:t1, :], g1[:, 1, t0:t1, :], 1.0, None, ALU.add))
                link(dve.reciprocal(g1[:, 1, t0:t1, :], g1[:, 2, t0:t1, :]))
                link(tt(g1[:, 0, t0:t1, :], g1[:, 1, t0:t1, :], rows[:, 16:24].unsqueeze(1).to_broadcast([P, t, E1]),
                        ALU.add))
                pick(g1[:, 0, t0:t1, :], g1s[:, 0, t0:t1], g1[:, 2, t0:t1, :], g1[:, 3, t0:t1, :], t, E1)

            def second_choice(t0, t1):
                without(g1[:, 0, t0:t1, :], g1[:, 3, t0:t1, :], g1[:, 0, t0:t1, :])
                pick(g1[:, 0, t0:t1, :], g1s[:, 0, t0:t1], g1[:, 2, t0:t1, :], g1[:, 4, t0:t1, :], t1 - t0, E1)
                link(tt(g1[:, 3, t0:t1, :], g1[:, 3, t0:t1, :], g1[:, 4, t0:t1, :], ALU.add))

            def combine_l1(t0, t1):
                t = t1 - t0
                chosen, score, work = g1[:, 3, t0:t1, :], g1[:, 1, t0:t1, :], g1[:, 2, t0:t1, :]
                low = g1[:, 4, t0:t1, :]
                denom, inverse, over, half = (g1s[:, k, t0:t1] for k in range(1, 5))
                link(tt(work, chosen, score, ALU.mult))
                link(dve.tensor_reduce(denom, work, AX, ALU.add))
                link(dve.tensor_scalar(over, denom, 1e-9, None, ALU.is_gt))
                link(dve.tensor_scalar(half, denom, 1e-9, None, ALU.add))
                link(dve.reciprocal(inverse, half))
                link(tt(inverse, inverse, over, ALU.mult))
                link(dve.tensor_scalar(half, over, -0.5, 0.5, ALU.mult, ALU.add))
                link(tt(work, work, wide(inverse, t, E1), ALU.mult))
                link(tt(low, chosen, wide(half, t, E1), ALU.mult))
                link(tt(work, work, low, ALU.add))

            def parts_l1(t0, t1):
                work, low = g1[:, 2, t0:t1, :], g1[:, 4, t0:t1, :]
                link(dve.tensor_copy(gparts[:, t0:t1, 0, :], work))
                link(tt(low, work, gparts[:, t0:t1, 0, :], ALU.subtract))
                link(dve.tensor_copy(gparts[:, t0:t1, 1, :], low))
                link(tt(work, low, gparts[:, t0:t1, 1, :], ALU.subtract))
                dve.tensor_copy(gparts[:, t0:t1, 2, :], work).then_inc(gparts_ready, 1)

            def last_hooks(p):
                if p == 3:
                    logits_l1(0, L - TB, m[:, 1, :], 1)
                if p == 5:
                    scores_l1(0, L - TB, 1)
                if p == 6:
                    second_choice(0, L - TB)
                if p == 7:
                    combine_l1(0, L - TB)
                if p == 8:
                    parts_l1(0, L - TB)

            def gate_routed(b, p):
                buf = p % 2
                dve.wait_ge(gb_ready, b.routed + (p - 1))
                dve.wait_ge(h_ready, b.pairs + (p + 1))
                for j in range(2):
                    tt(h[:, buf, j, :], h[:, buf, j, :], m[:, j, :], ALU.mult).then_inc(gated, 1)
                for j in range(2):
                    dve.wait_ge(ghi_done, b.chunks + (2 * (p - 2) + j + 1))
                    last = tt(hlo[:, buf, j, :], h[:, buf, j, :], hhi[:, buf, j, :].bitcast(F32), ALU.subtract)
                last.then_inc(split_done, 1)

            def gate_shared(b, p):
                buf = p % 2
                dve.wait_ge(h_ready, b.pairs + (p + 1))
                dve.wait_ge(z_ready, b.pairs * 2 + (2 * p + 2))
                dve.scalar_tensor_tensor(out=h[:, buf, 1, :], in0=h[:, buf, 0, :], scalar=1.0, in1=z[:, 2 * buf, :],
                                         op0=ALU.add, op1=ALU.mult).then_inc(half_gated, 1)
                dve.wait_ge(half_gated, b.shared + (p + 1))
                dve.scalar_tensor_tensor(out=h[:, buf, 0, :], in0=h[:, buf, 1, :], scalar=0.5,
                                         in1=z[:, 2 * buf + 1, :], op0=ALU.mult, op1=ALU.mult).then_inc(swiglu, 1)
                dve.wait_ge(swiglu, b.shared + (p + 1))
                dve.wait_ge(mm2_done, b.pairs + (p - 1))
                dve.tensor_copy(hhi[:, buf, 0, :], h[:, buf, 0, :]).then_inc(hi_dve, 1)
                dve.wait_ge(hi_dve, b.halves + (p + 1))
                tt(hlo[:, buf, 0, :], h[:, buf, 0, :], hhi[:, buf, 0, :].bitcast(F32),
                   ALU.subtract).then_inc(split_done, 1)

            def close_l1(pairs, number, columns):
                dve.wait_ge(mm2_done, pairs)
                dve.wait_ge(bank_read, number)
                dve.scalar_tensor_tensor(out=x2T, in0=y[:, 0, :], scalar=1.0 / 3.0, in1=xT[:, columns],
                                         op0=ALU.mult, op1=ALU.add).then_inc(y_used, 1)

            def l1_block(b, before=None, hooks=None):
                for p in range(L1_PAIRS):
                    if p < C1:
                        gate_shared(b, p)
                    else:
                        gate_routed(b, p)
                    if p == 0 and not b.first:
                        close_l1(b.pairs, b.index, b.shifted(-1))
                    if before is not None and p == 0:
                        job_out(before, len(JOBS[before.kind]) - 1, before.columns)
                    if before is not None and p == 1:
                        close_l0(before)
                    if hooks:
                        hooks(p)

            def first_l1_hooks(p):
                if p == 3:
                    logits_l1(L - TB, L, y[:, 1, :], 2)
                if p == 5:
                    scores_l1(L - TB, L, 2)
                    second_choice(L - TB, L)
                    combine_l1(L - TB, L)
                    parts_l1(L - TB, L)

            def w_split(e, lo, hi):
                link(dve.tensor_copy(whi[:, e, lo:hi], raw[:, e, lo:hi]))
                return tt(wlo[:, e, lo:hi], raw[:, e, lo:hi], whi[:, e, lo:hi].bitcast(F32), ALU.subtract)

            dve.wait_ge(w_in[SH], 32)
            w_split(SH, 0, 2 * H0).then_inc(w_ready, 1)
            x_copy(slice(0, BW), 1)
            dve.wait_ge(bT_turned, 1)
            dve.tensor_copy(bT[:, :], y[:, 0, 0:21]).then_inc(bT_ready, 1)
            dve.wait_ge(w_in[0], 32)
            w_split(0, 0, 2 * H0).then_inc(w_ready, 1)
            cond_prepare()
            dve.wait_ge(consts, 19)
            dve.tensor_copy(rhi[:, :], rw[:, 0, :]).then_inc(r_ready, 1)
            dve.wait_ge(r_ready, 1)
            tt(rlo[:, :], rw[:, 0, :], rhi[:, :].bitcast(F32), ALU.subtract).then_inc(r_ready, 1)
            l0_block(Block("mixed", 0, first=True), None, True, first_hooks)
            with dve.Fori(0, NBM - 1) as r:
                l0_block(Block("mixed", 1, r), Block("mixed", 0, r), True)
            l0_block(Block("proprio", NBM), Block("mixed", NBM - 1), True)
            l0_block(Block("proprio", NBM + 1), Block("proprio", NBM), True)
            l0_block(Block("proprio", NB - 1), Block("proprio", NB - 2), False, last_hooks)
            l1_block(Block("l1", 0, first=True), Block("proprio", NB - 1), first_l1_hooks)
            with dve.Fori(0, NB - 2) as r:
                l1_block(Block("l1", 1, r))
            l1_block(Block("l1", NB - 1))
            close_l1(L0_PAIRS + L1_PAIRS * NB, NB, slice((NB - 1) * BW, NB * BW))


_L0 = ["gate_w", "gate_b", "time_w", "time_b", "ew1", "eb1", "ew2", "eb2", "sw1", "sb1", "sw2", "sb2"]
_L1 = ["router_W", "router_bias", "w1", "w3", "w2", "W1e", "W2e"]
_INS = ["x", "cond_1024"] + ["L0_cond_" + n for n in _L0] + ["L1_cond_" + n for n in _L1]
_OUTS = [((P, L, P), "float32")]


def kernel(**inputs):
    import numpy as _np
    import concourse.bacc as _bacc
    from concourse import mybir as _mybir
    from concourse.bass_utils import run_bass_kernel_spmd as _run

    nc = _bacc.Bacc("TRN2", target_bir_lowering=False, num_devices=1)
    arrays, args = {}, []
    for name in _INS:
        a = _np.ascontiguousarray(inputs[name])
        arrays[f"in_{name}_dram"] = a
        args.append(nc.dram_tensor(f"in_{name}_dram", a.shape, _mybir.dt.from_np(a.dtype), kind="ExternalInput").ap())
    for i, (shape, dtype) in enumerate(_OUTS):
        dt = _mybir.dt.from_np(_np.dtype(dtype))
        args.append(nc.dram_tensor(f"out_{i}_dram", shape, dt, kind="ExternalOutput").ap())
    build(nc, *args)
    r = _run(nc, [arrays], core_ids=[0])
    return r.results[0]["out_0_dram"]
```

```python
from contextlib import ExitStack

import concourse.bass as bass
from concourse import mybir

ALU = mybir.AluOpType
ACT = mybir.ActivationFunctionType
AX = mybir.AxisListType.X
F32 = mybir.dt.float32
F32R = mybir.dt.float32r
BF16 = mybir.dt.bfloat16

P = 128
L = 32
LH = L // 3
LP = L - 2 * LH
E0, H0 = 4, 512
C0 = H0 // P
SH = E0
E1, HS1 = 8, 256
C1 = HS1 // P
TB = 4
BW = TB * P
HW = BW // 2
NB = L // TB
NBM = 2 * LH // TB
NBP = NB - NBM
BIG = 3.0e38

WHOLE = {e: [(e, 0, BW)] for e in (0, 1, 2, 3, SH)}
BOTH = [(1, 0, HW), (2, HW, BW)]
JOBS = {"mixed": [WHOLE[SH], WHOLE[0], WHOLE[3], BOTH],
        "proprio": [WHOLE[SH], WHOLE[0], WHOLE[1], WHOLE[2], WHOLE[3]]}
L0_PAIRS = 2 * (NBM * 4 + NBP * 5)
RUN = 2 * TB
RUNS = L // RUN
TURNS = {0: 1, 1: 2, 3: 3}
PEELED = max(TURNS) + 1
EARLY = L - RUN
L0_PARTS = NBM * 3 + NBP * 4
L1_PAIRS = C1 + E1 // 2
SELECT = 3 * E1

O_W1, O_W3, O_W2 = 0, HS1, 2 * HS1
O_W1E = O_W2 + C1 * P
O_W2E = O_W1E + E1 * P
N_L1W = O_W2E + E1 * P
L1_PIECES = ((0, O_W1E), (O_W1E, O_W2E), (O_W2E, N_L1W))


W_ORDER = ((SH, 1), (0, 1), (SH, 2), (0, 2), (3, 0), (1, 0), (2, 0))
W_COLUMNS = {0: slice(0, 2 * H0), 1: slice(0, H0), 2: slice(H0, 2 * H0)}


class Block:

    def __init__(self, kind, start, step=0, first=False):
        self.kind, self.first = kind, first
        self.index = step + start
        if kind == "mixed":
            self.pairs = step * 8 + 8 * start
            self.halves = step * 4 + 4 * start
            self.adds = step * 3 + 3 * start
        elif kind == "proprio":
            past = start - NBM
            self.pairs = step * 10 + (8 * NBM + 10 * past)
            self.halves = step * 5 + (4 * NBM + 5 * past)
            self.adds = step * 4 + (3 * NBM + 4 * past)
        else:
            self.pairs = step * L1_PAIRS + (L0_PAIRS + L1_PAIRS * start)
            self.shared = step * C1 + C1 * start
            self.routed = step * 4 + 4 * start
            self.chunks = step * E1 + E1 * start
        self.at = step * BW + start * BW
        self.columns = slice(self.at, self.at + BW) if isinstance(step, int) else bass.ds(self.at, BW)

    def shifted(self, by):
        at = self.at + by * BW
        return slice(at, at + BW) if isinstance(self.at, int) else bass.ds(at, BW)


def l0_last_adds(kind):
    return len(JOBS[kind]) - 1


def build(nc, x, cond, gate_w, gate_b, time_w, time_b, ew1, eb1, ew2, eb2, sw1, sb1, sw2, sb2,
          router_W, router_bias, w1, w3, w2, W1e, W2e, out):
    ctx = ExitStack()
    with ctx:
        def sb(name, shape, dt=F32):
            return ctx.enter_context(nc.sbuf_tensor("sb_" + name, shape, dt))

        def sem(name):
            return ctx.enter_context(nc.semaphore(name))

        z = ctx.enter_context(nc.psum_tensor("ps_z", [P, 4, BW], F32))
        y = ctx.enter_context(nc.psum_tensor("ps_y", [P, 2, BW], F32))
        m = ctx.enter_context(nc.psum_tensor("ps_m", [P, 2, BW], F32))
        y16, m16 = y[:, :, :].bitcast(BF16), m[:, :, :].bitcast(BF16)

        xnat = sb("xnat", [P, L, P])
        xstage = sb("xstage", [P, TB, P])
        xT = sb("xT", [P, L * P])
        xhi, xlo = sb("xhi", [P, L * P], F32R), sb("xlo", [P, L * P], F32R)
        raw = sb("raw", [P, E0 + 1, 2 * H0])
        whi, wlo = sb("whi", [P, E0 + 1, 2 * H0], F32R), sb("wlo", [P, E0 + 1, 2 * H0], F32R)
        raw1 = raw[:, :, :].rearrange("p e n -> p (e n)")[:, 0:N_L1W]
        vhi, vlo = sb("vhi", [P, N_L1W], F32R), sb("vlo", [P, N_L1W], F32R)
        h = sb("h", [P, 2, 2, BW])
        hhi, hlo = sb("hhi", [P, 2, 2, BW], F32R), sb("hlo", [P, 2, 2, BW], F32R)
        acc = sb("acc", [P, BW])
        part = sb("part", [P, 2, BW])
        ident = sb("ident", [P, P])
        ident16 = sb("ident16", [P, P], BF16)
        ones = sb("ones", [E0, P])
        mask3 = sb("mask3", [E0, 3])
        order = sb("order", [P, E1])
        select = sb("select", [SELECT, E1, P], BF16)
        brow = sb("brow", [21, P])
        bT = sb("bT", [P, 21])
        e2row = sb("e2row", [E0, P])
        vrow = sb("vrow", [1, 20])
        gw = sb("gw", [P, 3, E0])
        tw = sb("tw", [P, 2 * E0])
        rw = sb("rw", [P, 2, E1])
        rsplit = sb("rsplit", [P, 2, E1], F32R)
        cnat = sb("cnat", [P, P])
        csig = sb("csig", [P, 2, P])
        silu = sb("silu", [P, P])
        cT = sb("cT", [P, 2, P])
        sums = sb("sums", [P, 5, P])
        warm = sb("warm", [P, 2])
        agg = sb("agg", [P, 3, P])
        aggT = sb("aggT", [P, 3, P])
        rows = sb("rows", [P, 24])
        g0 = sb("g0", [P, 8, E0])
        g0s = sb("g0s", [P, 6])
        wbe = sb("wbe", [P, E0])
        wT = sb("wT", [E0, P])
        wdiag = sb("wdiag", [E0, E0, P])
        wmask = sb("wmask", [E0, 3, P])
        wb = sb("wb", [P, E0, P])
        base = sb("base", [P, 3, P])
        g1 = sb("g1", [P, 5, L, E1])
        g1s = sb("g1s", [P, 5, L])
        gparts = sb("gparts", [P, L, 3, E1], BF16)
        spare = xnat[:, :, :].rearrange("p l d -> p (l d)")
        gT = spare[0:SELECT, 0:L * P // 2].bitcast(BF16)
        x2T = spare[:, L * P // 2:L * P // 2 + BW]
        ostage = spare[:, L * P // 2 + BW:L * P // 2 + 2 * BW].rearrange("p (t d) -> p t d", t=TB)

        x_in, rows_in, gates_in = sem("x_in"), sem("rows_in"), sem("gates_in")
        xnat_in = [sem(f"xnat_in{k}") for k in range(3)]
        c_in, b_in = sem("c_in"), sem("b_in")
        w_in = [[sem(f"w{k}_in{e}") for k in (1, 2)] for e in range(E0 + 1)]
        v_in = sem("v_in")
        consts, late_consts, warm_ready = sem("consts"), sem("late_consts"), sem("warm_ready")
        x_turned = sem("x_turned")
        xhi_done, xT_done = sem("xhi_done"), sem("xT_done")
        x_ready = sem("x_ready")
        w_hi_done = sem("w_hi_done")
        w_ready = sem("w_ready")
        v_hi_done, v_ready = sem("v_hi_done"), sem("v_ready")
        r_ready = sem("r_ready")
        z_ready = sem("z_ready")
        h_ready = sem("h_ready")
        hi_act, hi_dve = sem("hi_act"), sem("hi_dve")
        split_done = sem("split_done")
        mm2_done = sem("mm2_done")
        part_ready = sem("part_ready")
        y_used = sem("y_used")
        part_weighted = sem("part_weighted")
        base_added = sem("base_added")
        adds_done = sem("adds_done")
        x1hi_done, x1_ready = sem("x1hi_done"), sem("x1_ready")
        half_gated, swiglu = sem("half_gated"), sem("swiglu")
        shared_hi = sem("shared_hi")
        gb_ready = sem("gb_ready")
        gated = sem("gated")
        ghi_done = sem("ghi_done")
        out_turned, stored = sem("out_turned"), sem("stored")
        bank_read = sem("bank_read")
        bT_turned, bT_ready = sem("bT_turned"), sem("bT_ready")
        c_tanh, c_turned, rows_mm, rows_ready = sem("c_tanh"), sem("c_turned"), sem("rows_mm"), sem("rows_ready")
        c_ready = sem("c_ready")
        silu_ready = sem("silu_ready")
        agg_ready, agg_turned, aggT_ready = sem("agg_ready"), sem("agg_turned"), sem("aggT_ready")
        logits0, shifted0, exp0 = sem("logits0"), sem("shifted0"), sem("exp0")
        wbe_ready, w_turned, wd_ready = sem("wbe_ready"), sem("w_turned"), sem("wd_ready")
        wb_mm, wb_ready = sem("wb_mm"), sem("wb_ready")
        logits1, logits1_ready, exp1 = sem("logits1"), sem("logits1_ready"), sem("exp1")
        gates_scaled = sem("gates_scaled")
        gparts_ready, g_turned, gT_ready = sem("gparts_ready"), sem("g_turned"), sem("gT_ready")
        pool_step = sem("pool_step")
        dve_step = sem("dve_step")

        block = ctx.enter_context(nc.Block())

        def hw(tensor):
            return tensor[:, 0:2 * LH, :].rearrange("p (s l) d -> p s l d", s=2)

        @block.sync
        def _(sp):
            def two_positions(tensor, at):
                return tensor[:, bass.ds(at, 2), :]

            def mixed(tensor, at):
                return hw(tensor)[:, :, bass.ds(at, TB // 2), :]

            def weights(e, layer):
                src = (sw1, sw2)[layer - 1] if e == SH else (ew1, ew2)[layer - 1][e]
                if layer == 2:
                    src = src.rearrange("(c h) d -> h c d", c=C0)
                sp.dma_start(raw[:, e, W_COLUMNS[layer]], src).then_inc(w_in[e][layer - 1], 16)

            sp.dma_start(hw(xnat)[:, :, 0:TB, :], hw(x)[:, :, 0:TB, :]).then_inc(xnat_in[0], 16)
            sp.dma_start(cnat[:, :], cond).then_inc(c_in, 16)
            weights(SH, 1)
            weights(SH, 2)
            weights(0, 1)
            sp.dma_start(hw(xnat)[:, :, TB:, :], hw(x)[:, :, TB:, :]).then_inc(xnat_in[1], 16)
            weights(0, 2)
            sp.dma_start(tw[:, :], time_w).then_inc(rows_in, 16)
            sp.dma_start(vrow[:, 4:12], time_b.rearrange("(a h) -> a h", a=1)).then_inc(rows_in, 16)
            sp.dma_start(rw[:, :, :], router_W.rearrange("(j p) e -> p j e", j=2)).then_inc(rows_in, 16)
            sp.dma_start(vrow[:, 12:20], router_bias.rearrange("(a h) -> a h", a=1)).then_inc(rows_in, 16)
            sp.dma_start(xnat[:, 2 * LH:, :], x[:, 2 * LH:, :]).then_inc(xnat_in[2], 16)
            sp.dma_start(gw[:, :, :], gate_w.rearrange("(j p) e -> p j e", j=3)).then_inc(gates_in, 16)
            sp.dma_start(vrow[:, 0:4], gate_b.rearrange("(a h) -> a h", a=1)).then_inc(gates_in, 16)
            for e in (3, 1, 2):
                weights(e, 1)
                weights(e, 2)
            staged = xstage[:, :, :].rearrange("p (s l) d -> p s l d", s=2)
            sp.dma_start(staged, mixed(x, TB)).then_inc(x_in, 16)
            sp.wait_ge(w_ready, len(W_ORDER))
            for at, n, src in ((O_W1, HS1, w1), (O_W3, HS1, w3),
                               (O_W2, C1 * P, w2.rearrange("(c h) d -> h c d", c=C1)),
                               (O_W1E, E1 * P, W1e.rearrange("e c h -> c e h")),
                               (O_W2E, E1 * P, W2e.rearrange("e h d -> h e d"))):
                sp.dma_start(raw1[:, at:at + n], src).then_inc(v_in, 16)
            with sp.Fori(0, NBM - 3) as r:
                sp.wait_ge(x_turned, r + 3)
                sp.dma_start(staged, mixed(x, r * 2 + 6)).then_inc(x_in, 16)
            with sp.Fori(0, NBP) as r:
                sp.wait_ge(x_turned, r + NBM)
                sp.dma_start(xstage[:, :, :], x[:, bass.ds(r * TB + 2 * LH, TB), :]).then_inc(x_in, 16)

            def store(first, second, copied):
                sp.wait_ge(bank_read, copied + 1)
                sp.dma_start(two_positions(out, first), ostage[:, 0:2, :]).then_inc(stored, 16)
                sp.dma_start(two_positions(out, second), ostage[:, 2:4, :]).then_inc(stored, 16)

            with sp.Fori(0, NBM) as r:
                store(r * 2, r * 2 + LH, r + 1)
            with sp.Fori(0, NBP) as r:
                store(r * 4 + 2 * LH, r * 4 + (2 * LH + 2), r + (NBM + 1))
            sp.wait_ge(stored, 32 * NB)

        @block.gpsimd
        def _(pool):
            pool.memset(warm[:, 0:1], 0.0).then_inc(warm_ready, 1)
            pool.memset(ident[:, :], 0.0).then_inc(consts, 1)
            pool.memset(mask3[:, :], 1.0).then_inc(consts, 1)
            pool.memset(ones[:, :], 1.0).then_inc(consts, 1)
            for e in range(E1):
                pool.memset(order[:, e:e + 1], float(E1 - e)).then_inc(consts, 1)
            pool.wait_ge(consts, 3 + E1)

            def diagonal(tile):
                return pool.affine_select(out=tile[:, :], in_=tile[:, :], compare_op=ALU.not_equal, fill=1.0,
                                          base=0, pattern=[[-1, P]], channel_multiplier=1)

            diagonal(ident).then_inc(consts, 1)
            pool.affine_select(out=mask3[:, 0:2], in_=mask3[:, 0:2], compare_op=ALU.not_equal, fill=0.0,
                               base=-2, pattern=[[1, 2]], channel_multiplier=1).then_inc(consts, 1)
            for dst, src in ((brow[16:20, :], sb1.rearrange("(c h) -> c h", c=C0)),
                             (brow[0:16, :], eb1.rearrange("e (c h) -> (e c) h", c=C0)),
                             (brow[20:21, :], sb2.rearrange("(a h) -> a h", a=1)), (e2row[:, :], eb2)):
                pool.dma_start(dst, src).then_inc(b_in, 16)

            def l1_constants():
                pool.memset(ident16[:, :], 0.0).then_inc(late_consts, 1)
                pool.memset(select[:, :, :], 0.0).then_inc(late_consts, 1)
                pool.wait_ge(late_consts, 2)
                diagonal(ident16).then_inc(late_consts, 1)
                for k in range(3):
                    pool.wait_ge(late_consts, 3 + k)
                    pool.affine_select(out=select[:, :, :], in_=select[:, :, :], compare_op=ALU.not_equal,
                                       fill=1.0, base=-E1 * k, pattern=[[-1, E1], [0, P]],
                                       channel_multiplier=1).then_inc(late_consts, 1)

            def x_lo(b, columns, number):
                pool.wait_ge(xhi_done, number)
                pool.tensor_tensor(xlo[:, columns], xT[:, columns], xhi[:, columns].bitcast(F32),
                                   ALU.subtract).then_inc(x_ready, 1)

            def w_lo(n):
                e, columns = W_ORDER[n][0], W_COLUMNS[W_ORDER[n][1]]
                pool.wait_ge(w_hi_done, n + 1)
                pool.tensor_tensor(wlo[:, e, columns], raw[:, e, columns], whi[:, e, columns].bitcast(F32),
                                   ALU.subtract).then_inc(w_ready, 1)

            def v_lo(n):
                at, end = L1_PIECES[n]
                pool.wait_ge(v_hi_done, n + 1)
                pool.tensor_tensor(vlo[:, at:end], raw1[:, at:end], vhi[:, at:end].bitcast(F32),
                                   ALU.subtract).then_inc(v_ready, 1)

            def add_base(b):
                pool.wait_ge(y_used, b.index + 1)
                pool.wait_ge(wb_ready, 2)
                if b.first:
                    pool.wait_ge(adds_done, 2)
                if b.kind == "mixed":
                    other = base[:, 0:2, :].unsqueeze(2).to_broadcast([P, 2, 2, P])
                    own = acc[:, :].rearrange("p (a b c) -> p a b c", a=2, b=2)
                else:
                    other = base[:, 2, :].unsqueeze(1).to_broadcast([P, TB, P])
                    own = acc[:, :].rearrange("p (b c) -> p b c", b=TB)
                pool.tensor_tensor(own, own, other, ALU.add).then_inc(base_added, 1)

            def add_part(b, j):
                pool.wait_ge(part_ready, b.adds + j)
                if b.first:
                    pool.wait_ge(*((y_used, 1) if j == 1 else (adds_done, 1) if j == 2 else (base_added, 1)))
                elif j == 1:
                    pool.wait_ge(base_added, b.index + 1)
                else:
                    pool.wait_ge(adds_done, b.adds + (j - 1))
                pool.tensor_tensor(acc[:, :], acc[:, :], part[:, j % 2, :], ALU.add).then_inc(adds_done, 1)

            def weight_part(b, j):
                pool.wait_ge(part_ready, j)
                pool.wait_ge(wb_ready, 1)
                own = part[:, j % 2, :].rearrange("p (b c) -> p b c", b=TB)
                weights = wb[:, JOBS[b.kind][j][0][0], :].unsqueeze(1).to_broadcast([P, TB, P])
                pool.tensor_tensor(own, own, weights, ALU.mult).then_inc(part_weighted, 1)
                pool.wait_ge(part_weighted, j)

            def l0_block(b, next_x, hooks=None):
                if b.first:
                    x_lo(b, b.shifted(1), 2)
                    for j in (1, 2):
                        weight_part(b, j)
                        add_part(b, j)
                    add_base(b)
                    add_part(b, 3)
                    return
                for j in range(len(JOBS[b.kind])):
                    if j == 0:
                        add_base(b)
                    else:
                        add_part(b, j)
                    if j == 1 and next_x:
                        x_lo(b, b.shifted(1), b.index + 2)
                    if hooks:
                        hooks(j)

            steps = [0]

            def link(ins):
                steps[0] += 1
                ins.then_inc(pool_step, 1)
                pool.wait_ge(pool_step, steps[0])

            def finish_gates(run):
                at = slice(run * RUN, (run + 1) * RUN)
                work, chosen, low = (g1[:, k, at, :] for k in (2, 3, 4))
                inverse, half = (g1s[:, k, at].unsqueeze(2).to_broadcast([P, RUN, E1]) for k in (2, 4))
                pool.wait_ge(gates_scaled, 1 if run < RUNS - 1 else 2)
                link(pool.tensor_tensor(work, work, inverse, ALU.mult))
                link(pool.tensor_tensor(low, chosen, half, ALU.mult))
                link(pool.tensor_tensor(work, work, low, ALU.add))
                link(pool.tensor_copy(gparts[:, at, 0, :], work))
                link(pool.tensor_tensor(low, work, gparts[:, at, 0, :], ALU.subtract))
                link(pool.tensor_copy(gparts[:, at, 1, :], low))
                link(pool.tensor_tensor(work, low, gparts[:, at, 1, :], ALU.subtract))
                pool.tensor_copy(gparts[:, at, 2, :], work).then_inc(gparts_ready, 1)

            for n in range(len(W_ORDER)):
                w_lo(n)
            l1_constants()
            l0_block(Block("mixed", 0, first=True), True)
            with pool.Fori(0, NBM - 1) as r:
                l0_block(Block("mixed", 1, r), True)
            l0_block(Block("proprio", NBM), True)
            l0_block(Block("proprio", NBM + 1), True, lambda j: v_lo(j - 1) if 1 <= j <= 3 else None)

            l0_block(Block("proprio", NB - 1), False, lambda j: finish_gates(0) if j == 2 else None)
            for run in range(1, RUNS):
                finish_gates(run)

        @block.scalar
        def _(act):
            def x_hi(columns, number):
                act.wait_ge(xT_done, number)
                act.activation(xhi[:, columns], xT[:, columns], ACT.Copy).then_inc(xhi_done, 1)

            def w_hi(n):
                e, layer = W_ORDER[n]
                for k in (1, 2) if layer == 0 else (layer,):
                    act.wait_ge(w_in[e][k - 1], 16)
                columns = W_COLUMNS[layer]
                act.activation(whi[:, e, columns], raw[:, e, columns], ACT.Copy).then_inc(w_hi_done, 1)

            def hidden_l0(b, p):
                buf = p % 2
                for j in range(2):
                    c = 2 * (p % 2) + j
                    act.wait_ge(z_ready, b.pairs * 2 + (2 * p + j + 1))
                    if j == 0 and not (b.first and p < 2):
                        act.wait_ge(split_done, b.pairs + (p - 1))
                    for e, lo, hi in JOBS[b.kind][p // 2]:
                        last = act.activation(h[:, buf, j, lo:hi], z[:, 2 * buf + j, lo:hi],
                                              ACT.Gelu_apprx_tanh, bias=bT[:, C0 * e + c:C0 * e + c + 1])
                last.then_inc(h_ready, 1)
                if p % 2 == 0:
                    act.wait_ge(h_ready, b.pairs + (p + 1))
                    if not (b.first and p < 2):
                        act.wait_ge(mm2_done, b.pairs + (p - 1))
                    act.activation(hhi[:, buf, :, :], h[:, buf, :, :], ACT.Copy).then_inc(hi_act, 1)

            def l0_block(b, next_x, hooks=None):
                for p in range(2 * len(JOBS[b.kind])):
                    hidden_l0(b, p)
                    if p == 4 and next_x:
                        x_hi(b.shifted(1), b.index + 2)
                    if hooks:
                        hooks(p)

            def first_hooks(p):
                if p < 4:
                    w_hi(p + 3)
                if p == 4:
                    act.wait_ge(shifted0, 2)
                    act.activation(g0[:, 2, :], g0[:, 1, :], ACT.Exp, bias=g0s[:, 0:1],
                                   accum_out=g0s[:, 1:2]).then_inc(exp0, 1)

            def sixth_hooks(p):
                if p < 3:
                    at, end = L1_PIECES[p]
                    act.wait_ge(v_in, 16 * 5)
                    act.activation(vhi[:, at:end], raw1[:, at:end], ACT.Copy).then_inc(v_hi_done, 1)
                if p == 4:
                    exp_router(0, EARLY, 1)

            def last_hooks(p):
                if p == 9:
                    act.activation(warm[:, 1:2], warm[:, 0:1], ACT.Gelu)
                    turned_gates(0)

            def exp_router(t0, t1, number):
                act.wait_ge(*((logits1_ready, 1) if number == 1 else (bank_read, 1)))
                act.activation(g1[:, 1, t0:t1, :], g1[:, 0, t0:t1, :], ACT.Exp, scale=-1.0).then_inc(exp1, 1)

            def gated_hi(b, p, before):
                for j in range(2):
                    n = b.chunks + (2 * (p - 2) + j + 1 - (E1 if before else 0))
                    act.wait_ge(gated, n)
                    if j == 0:
                        act.wait_ge(mm2_done, b.pairs + (p - 1 - (L1_PAIRS if before else 0)))
                    act.activation(hhi[:, p % 2, j, :], h[:, p % 2, j, :], ACT.Copy).then_inc(ghi_done, 1)

            def copy_out(number):
                act.wait_ge(out_turned, number)
                if not (isinstance(number, int) and number == 1):
                    act.wait_ge(stored, (number - 1) * 32)
                act.activation(ostage, y[:, 1, :].rearrange("p (t d) -> p t d", t=TB),
                               ACT.Copy).then_inc(bank_read, 1)

            def shared_chunk_hi(b, p):
                act.wait_ge(swiglu, b.shared + (p + 1))
                act.wait_ge(mm2_done, b.pairs + (p - 1))
                act.activation(hhi[:, p, 0, :], h[:, p, 0, :], ACT.Copy).then_inc(shared_hi, 1)

            def l1_block(b, hooks=None):
                for p in range(L1_PAIRS):
                    buf = p % 2
                    if p == 0 and not b.first:
                        gated_hi(b, L1_PAIRS - 1, True)
                    if p > 2:
                        gated_hi(b, p - 1, False)
                    act.wait_ge(split_done, b.pairs + (p - 1))
                    if p < C1:
                        act.wait_ge(z_ready, b.pairs * 2 + (2 * p + 1))
                        act.activation(h[:, buf, 0, :], z[:, 2 * buf, :], ACT.Tanh, scale=0.5).then_inc(h_ready, 1)
                    else:
                        act.wait_ge(z_ready, b.pairs * 2 + (2 * p + 2))
                        act.activation(h[:, buf, :, :], z[:, 2 * buf:2 * buf + 2, :], ACT.Gelu).then_inc(h_ready, 1)
                    if p == 1:
                        shared_chunk_hi(b, 0)
                        shared_chunk_hi(b, 1)
                    if p == 3 and not b.first:
                        copy_out(b.index)
                    if hooks:
                        hooks(p)

            def turned_gates(k):
                act.wait_ge(g_turned, k + 1)
                src = m16[0:SELECT, 0, :] if k == 0 else y16[0:SELECT, 1, :]
                act.activation(gT[:, k * RUN * P:(k + 1) * RUN * P], src, ACT.Copy).then_inc(gT_ready, 1)

            act.wait_ge(warm_ready, 1)
            act.activation(warm[:, 1:2], warm[:, 0:1], ACT.Gelu_apprx_tanh)
            act.wait_ge(c_in, 16)
            act.activation(csig[:, 0, :], cnat[:, :], ACT.Tanh, scale=0.5).then_inc(c_tanh, 1)
            w_hi(0)
            x_hi(slice(0, BW), 1)
            w_hi(1)
            w_hi(2)
            act.wait_ge(bT_ready, 1)
            l0_block(Block("mixed", 0, first=True), True, first_hooks)
            with act.Fori(0, NBM - 1) as r:
                l0_block(Block("mixed", 1, r), True)
            l0_block(Block("proprio", NBM), True)
            l0_block(Block("proprio", NBM + 1), True, sixth_hooks)
            l0_block(Block("proprio", NB - 1), False, last_hooks)

            def early_hooks(k):
                def hooks(p):
                    if p == L1_PAIRS - 1 and k in TURNS:
                        turned_gates(TURNS[k])
                    if k == 1 and p == 5:
                        exp_router(EARLY, L, 2)
                return hooks

            for k in range(PEELED):
                l1_block(Block("l1", k, first=k == 0), early_hooks(k))
            with act.Fori(0, NB - PEELED) as r:
                l1_block(Block("l1", PEELED, r))
            gated_hi(Block("l1", NB), L1_PAIRS - 1, True)
            copy_out(NB)

        @block.tensor
        def _(pe):
            def three(dst, hi, lo, rhs_hi, rhs_lo, start, stop, **kw):
                pe.matmul(dst, hi, rhs_hi, start=start, stop=False, **kw)
                pe.matmul(dst, lo, rhs_hi, start=False, stop=False, **kw)
                return pe.matmul(dst, hi, rhs_lo, start=False, stop=stop, **kw)

            def turn_x(number, positions=None):
                if positions is None:
                    pe.wait_ge(wb_ready, 2)
                    pe.wait_ge(x_in, number * 16 - 32)
                    pe.wait_ge(xT_done, number - 1)
                for t in range(TB):
                    src = xstage[:, t, :] if positions is None else xnat[:, positions[t], :]
                    last = pe.transpose(m[:, 0, t * P:(t + 1) * P], src, ident[:, :])
                last.then_inc(x_turned, 1)

            def first_layer_l0(b, p, by=0):
                buf = p % 2
                if not (b.first and p < 2 and not by):
                    pe.wait_ge(h_ready, b.pairs + (p - 1))
                if p == 0:
                    pe.wait_ge(x_ready, b.index + 1)
                for j in range(2):
                    c = 2 * (p % 2) + j
                    for e, lo, hi in JOBS[b.kind][p // 2]:
                        cols = bass.ds(b.at + lo, hi - lo)
                        last = three(z[:, 2 * buf + j, lo:hi], whi[:, e, c * P:(c + 1) * P],
                                     wlo[:, e, c * P:(c + 1) * P], xhi[:, cols], xlo[:, cols], True, True)
                    last.then_inc(z_ready, 1)

            def second_layer_l0(b, p):
                n_jobs = len(JOBS[b.kind])
                j0, buf = p // 2, p % 2
                bank = (n_jobs - 1 - j0) % 2
                pe.wait_ge(split_done, b.pairs + (p + 1))
                if p % 2 == 0:
                    if j0 == 2:
                        pe.wait_ge(y_used, b.index + 1)
                    elif j0 > 2:
                        pe.wait_ge(part_ready, b.adds + (j0 - 2))
                    elif not b.first:
                        pe.wait_ge(part_ready, b.adds)
                segments = JOBS[b.kind][j0]
                for j in range(2):
                    c = 2 * (p % 2) + j
                    for n, (e, lo, hi) in enumerate(segments):
                        at = H0 + c * P
                        last = three(y[:, bank, lo:hi], whi[:, e, at:at + P], wlo[:, e, at:at + P],
                                     hhi[:, buf, j, lo:hi], hlo[:, buf, j, lo:hi],
                                     c == 0 and n == 0, c == C0 - 1, skip_group_check=len(segments) > 1)
                last.then_inc(mm2_done, 1)

            def l0_block(b, following, next_x, hooks=None):
                n = 2 * len(JOBS[b.kind])
                for p in range(n):
                    if b.first and p % 2 == 0 and p + 2 < n:
                        pe.wait_ge(w_ready, {0: 2, 2: 5, 4: 7}[p])
                    if p + 2 < n:
                        first_layer_l0(b, p + 2)
                    else:
                        following(p + 2 - n)
                    if b.first and p in (0, 2):
                        pe.wait_ge(w_ready, 3 if p == 0 else 4)
                    second_layer_l0(b, p)
                    if p == 1 and b.first:
                        pe.wait_ge(xT_done, 1)
                        turn_x(2, (2, 3, LH + 2, LH + 3))
                    elif p == 1 and next_x:
                        turn_x(b.index + 2)
                    if hooks:
                        hooks(p)

            def turn_cond():
                pe.wait_ge(silu_ready, 1)
                pe.transpose(m[:, 1, 0:P], silu[:, :], ident[:, :])
                pe.transpose(m[:, 1, P:2 * P], cnat[:, :], ident[:, :]).then_inc(c_turned, 1)

            def gate_rows():
                pe.wait_ge(rows_in, 16 * 4)
                pe.wait_ge(c_ready, 1)
                pe.matmul(m[:, 1, 384:392], cT[:, 0, :], tw[:, :], start=True, stop=False)
                pe.matmul(m[:, 1, 384:392], ones[0:1, :], vrow[:, 4:12], start=False, stop=True)
                pe.matmul(m[:, 1, 392:400], cT[:, 1, :], rw[:, 1, :], start=True, stop=True)
                pe.matmul(m[:, 1, 400:408], ones[0:1, :], vrow[:, 12:20], start=True, stop=True).then_inc(rows_mm, 1)

            def gate_means():
                pe.wait_ge(rows_ready, 1)
                pe.wait_ge(agg_ready, 2)
                for j in range(3):
                    last = pe.transpose(m[:, 1, j * P:(j + 1) * P], agg[:, j, :], ident[:, :])
                last.then_inc(agg_turned, 1)

            def gate_logits():
                pe.wait_ge(gates_in, 16 * 2)
                pe.wait_ge(aggT_ready, 2)
                for j in range(3):
                    pe.matmul(m[:, 1, 408:412], aggT[:, j, :], gw[:, j, :], start=j == 0, stop=False)
                pe.matmul(m[:, 1, 408:412], ones[0:1, :], vrow[:, 0:4], start=False, stop=True).then_inc(logits0, 1)

            def first_hooks(p):
                if p == 0:
                    gate_rows()
                if p == 1:
                    gate_means()
                if p == 2:
                    gate_logits()
                if p == 6:
                    pe.wait_ge(wbe_ready, 1)
                    pe.matmul(m[0:E0, 1, 0:P], wbe[:, :], ident[:, :], start=True, stop=True).then_inc(w_turned, 1)
                if p == 7:
                    pe.wait_ge(wd_ready, 2)
                    pe.matmul(m[:, 1, :], ones[:, :], wdiag[:, :, :].rearrange("k e b -> k (e b)"),
                              start=True, stop=True).then_inc(wb_mm, 1)
                    pe.wait_ge(xT_done, 2)
                    pe.matmul(m[:, 0, 0:3 * P], e2row[:, :], wmask[:, :, :].rearrange("k e b -> k (e b)"),
                              start=True, stop=True).then_inc(wb_mm, 1)

            def route(block, dst, first):
                pe.wait_ge(x1_ready, 2 * (block + 1))
                for t in range(block * TB, (block + 1) * TB):
                    at = slice(t * P, (t + 1) * P)
                    to = (t - first) * 2 * E1
                    pe.matmul(dst[:, to:to + 2 * E1], xhi[:, at], rsplit[:, :, :].rearrange("p k e -> p (k e)"),
                              start=True, stop=False, skip_group_check=True)
                    last = pe.matmul(dst[:, to:to + E1], xlo[:, at], rsplit[:, 0, :],
                                     start=False, stop=True, skip_group_check=True)
                return last

            def turn_gates(k):
                dst = m16[0:SELECT, 0, :] if k == 0 else y16[0:SELECT, 1, :]
                pe.wait_ge(gparts_ready, k + 1)
                for t in range(RUN):
                    last = pe.transpose(dst[:, t * P:(t + 1) * P],
                                        gparts[:, k * RUN + t, :, :].rearrange("p k e -> p (k e)"), ident16[:, :])
                last.then_inc(g_turned, 1)

            def fifth_hooks(p):
                if p == 2:
                    pe.wait_ge(r_ready, 2)
                if 2 <= p < 2 + NBM:
                    route(p - 2, m[:, 1, :], 0)

            def sixth_hooks(p):
                if p == 2:
                    route(NBM, m[:, 1, :], 0).then_inc(logits1, 1)

            def last_hooks(p):
                if p == 8:
                    pe.wait_ge(late_consts, 6)
                    pe.wait_ge(xT_done, NB)
                    turn_gates(0)

            def first_layer_l1(b, p, gates=None):
                buf = p % 2
                if p in (2, 3):
                    pe.wait_ge(swiglu, b.shared + (p - 1))
                else:
                    pe.wait_ge(h_ready, b.pairs + (p - 1))
                if gates and not (gates[0].first and gates[1] == 2):
                    pe.wait_ge(gated, gates[0].chunks + 2 * (gates[1] - 2))
                if b.first and p in (0, 2):
                    pe.wait_ge(v_ready, 1 if p == 0 else 2)
                if p < 2:
                    offsets = (O_W1 + p * P, O_W3 + p * P)
                else:
                    offsets = tuple(O_W1E + (2 * (p - 2) + j) * P for j in range(2))
                for j, at in enumerate(offsets):
                    three(z[:, 2 * buf + j, :], vhi[:, at:at + P], vlo[:, at:at + P],
                          xhi[:, b.columns], xlo[:, b.columns], True, True).then_inc(z_ready, 1)
                    if gates and j == 0:
                        gates_out(*gates)

            def gates_out(b, p):
                for j in range(2):
                    last = pe.matmul(m[:, j, :], select[:, 2 * (p - 2) + j, :], gT[:, b.columns],
                                     start=True, stop=True)
                last.then_inc(gb_ready, 1)

            def second_layer_l1(b, p):
                buf = p % 2
                if p == 2 and b.first:
                    pe.wait_ge(v_ready, 3)
                if p == 0 and b.first:
                    pe.wait_ge(part_ready, L0_PARTS)
                elif p == 0:
                    pe.wait_ge(y_used, b.index + NB)
                pe.wait_ge(split_done, b.pairs + (p + 1))
                if p < 2:
                    at = O_W2 + p * P
                    last = three(y[:, 0, :], vhi[:, at:at + P], vlo[:, at:at + P],
                                 hhi[:, buf, 0, :], hlo[:, buf, 0, :], p == 0, False)
                else:
                    for j in range(2):
                        at = O_W2E + (2 * (p - 2) + j) * P
                        last = three(y[:, 0, :], vhi[:, at:at + P], vlo[:, at:at + P],
                                     hhi[:, buf, j, :], hlo[:, buf, j, :], False, p == L1_PAIRS - 1 and j == 1)
                last.then_inc(mm2_done, 1)

            def turn_out(number):
                turned = [run for k, run in TURNS.items() if not isinstance(number, int) or k < number]
                pe.wait_ge(gT_ready, max(turned) + 1)
                pe.wait_ge(y_used, number + NB)
                pe.wait_ge(bank_read, number)
                for t in range(TB):
                    last = pe.transpose(y[:, 1, t * P:(t + 1) * P], x2T[:, t * P:(t + 1) * P], ident[:, :])
                last.then_inc(out_turned, 1)

            def l1_block(b, following=None, hooks=None):
                for p in range(L1_PAIRS):
                    if b.first and p == 1:
                        pe.wait_ge(gT_ready, 1)
                    gates = (b, p + 1) if 2 <= p + 1 < L1_PAIRS else None
                    if p + 2 < L1_PAIRS:
                        first_layer_l1(b, p + 2, gates)
                    elif following:
                        following(p + 2 - L1_PAIRS, gates)
                    elif gates:
                        pe.wait_ge(gated, b.chunks + 2 * (p - 1))
                        gates_out(*gates)
                    if p == 1:
                        second_layer_l1(b, 0)
                    if p > 0:
                        second_layer_l1(b, p)
                    if p == 1 and not b.first:
                        turn_out(b.index)
                    if hooks:
                        hooks(p)

            def keep_busy(n):
                for _ in range(n):
                    pe.matmul(z[:, 3, 0:P], ident[:, :], ident[:, :], start=True, stop=True)

            b = Block("mixed", 0, first=True)
            pe.wait_ge(consts, 5 + E1)
            keep_busy(4)
            pe.wait_ge(xnat_in[0], 16)
            turn_x(1, (0, 1, LH, LH + 1))
            turn_cond()
            keep_busy(4)
            pe.wait_ge(w_ready, 1)
            first_layer_l0(b, 0)
            pe.wait_ge(b_in, 16 * 4)
            pe.transpose(y[:, 0, 0:21], brow[:, :], ident[0:21, 0:21]).then_inc(bT_turned, 1)
            first_layer_l0(b, 1)
            pe.wait_ge(bT_ready, 1)
            l0_block(b, lambda p: first_layer_l0(Block("mixed", 1), p), True, first_hooks)
            with pe.Fori(0, NBM - 1) as r:
                l0_block(Block("mixed", 1, r), lambda p: first_layer_l0(Block("mixed", 2, r), p), True)
            for k, hooks in ((NBM, fifth_hooks), (NBM + 1, sixth_hooks)):
                l0_block(Block("proprio", k), lambda p, k=k: first_layer_l0(Block("proprio", k + 1), p), True, hooks)
            l0_block(Block("proprio", NB - 1), lambda p: first_layer_l1(Block("l1", 0, first=True), p),
                     False, last_hooks)

            def early_hooks(k):
                def hooks(p):
                    if p == 3 and k in TURNS:
                        if k:
                            pe.wait_ge(bank_read, k + 1)
                        turn_gates(TURNS[k])
                    if k == 0 and p == 5:
                        pe.wait_ge(gT_ready, 2)
                        route(NB - 2, y[:, 1, :], EARLY)
                        route(NB - 1, y[:, 1, :], EARLY).then_inc(logits1, 1)
                return hooks

            for k in range(PEELED):
                l1_block(Block("l1", k, first=k == 0),
                         lambda p, g, k=k: first_layer_l1(Block("l1", k + 1), p, g), early_hooks(k))
            with pe.Fori(0, NB - 1 - PEELED) as r:
                l1_block(Block("l1", PEELED, r), lambda p, g: first_layer_l1(Block("l1", PEELED + 1, r), p, g))
            l1_block(Block("l1", NB - 1))
            turn_out(NB)

        @block.vector
        def _(dve):
            steps = [0]

            def link(ins):
                steps[0] += 1
                ins.then_inc(dve_step, 1)
                dve.wait_ge(dve_step, steps[0])

            def tt(out_, a, b_, op):
                return dve.tensor_tensor(out_, a, b_, op)

            def x_copy(columns, number):
                dve.wait_ge(x_turned, number)
                dve.tensor_copy(xT[:, columns], m[:, 0, :]).then_inc(xT_done, 1)

            def split_l0(b, p):
                buf = p % 2
                if p % 2 == 0:
                    dve.wait_ge(hi_act, b.halves + (p // 2 + 1))
                else:
                    dve.wait_ge(h_ready, b.pairs + (p + 1))
                    if not (b.first and p < 2):
                        dve.wait_ge(mm2_done, b.pairs + (p - 1))
                    dve.tensor_copy(hhi[:, buf, :, :], h[:, buf, :, :]).then_inc(hi_dve, 1)
                    dve.wait_ge(hi_dve, b.halves + (p // 2 + 1))
                tt(hlo[:, buf, :, :], h[:, buf, :, :], hhi[:, buf, :, :].bitcast(F32),
                   ALU.subtract).then_inc(split_done, 1)

            def job_out(b, j, columns):
                n_jobs = len(JOBS[b.kind])
                bank = (n_jobs - 1 - j) % 2
                dve.wait_ge(mm2_done, b.pairs + (2 * j + 2))
                if j == 0:
                    if not b.first:
                        dve.wait_ge(x1_ready, b.index * 2)
                    tt(acc[:, :], y[:, bank, :], xT[:, columns], ALU.add).then_inc(y_used, 1)
                    return
                if b.first and j < 3:
                    dve.tensor_copy(part[:, j % 2, :], y[:, bank, :]).then_inc(part_ready, 1)
                    return
                dve.wait_ge(wb_ready, 2)
                if j >= 3:
                    dve.wait_ge(adds_done, b.adds + (j - 2))
                if JOBS[b.kind][j] is BOTH:
                    weights = wb[:, 1:3, :].unsqueeze(2).to_broadcast([P, 2, 2, P])
                    shape = dict(a=2, b=2)
                    src = y[:, bank, :].rearrange("p (a b c) -> p a b c", **shape)
                    dst = part[:, j % 2, :].rearrange("p (a b c) -> p a b c", **shape)
                else:
                    e = JOBS[b.kind][j][0][0]
                    weights = wb[:, e, :].unsqueeze(1).to_broadcast([P, TB, P])
                    src = y[:, bank, :].rearrange("p (b c) -> p b c", b=TB)
                    dst = part[:, j % 2, :].rearrange("p (b c) -> p b c", b=TB)
                tt(dst, src, weights, ALU.mult).then_inc(part_ready, 1)

            def close_l0(b, steps=(0, 1)):
                if 0 in steps:
                    dve.wait_ge(adds_done, b.adds + l0_last_adds(b.kind))
                    dve.tensor_copy(xhi[:, b.columns], acc[:, :]).then_inc(x1hi_done, 1)
                    dve.tensor_copy(xT[:, b.columns], acc[:, :]).then_inc(x1_ready, 1)
                if 1 not in steps:
                    return
                dve.wait_ge(x1hi_done, b.index + 1)
                tt(xlo[:, b.columns], acc[:, :], xhi[:, b.columns].bitcast(F32),
                   ALU.subtract).then_inc(x1_ready, 1)

            def l0_block(b, before, next_x, hooks=None):
                n_jobs = len(JOBS[b.kind])
                for p in range(2 * n_jobs):
                    split_l0(b, p)
                    if p == 3 and next_x:
                        x_copy(b.shifted(1), b.index + 2)
                    if before is not None and p == 0:
                        job_out(before, len(JOBS[before.kind]) - 1, before.columns)
                    if before is not None and p == 1:
                        close_l0(before)
                    if hooks:
                        hooks(p)
                    if p >= 2 and p % 2 == 0:
                        job_out(b, p // 2 - 1, b.columns)

            def cond_prepare():
                dve.wait_ge(c_tanh, 1)
                link(dve.scalar_tensor_tensor(out=csig[:, 1, :], in0=csig[:, 0, :], scalar=1.0, in1=cnat[:, :],
                                              op0=ALU.add, op1=ALU.mult))
                dve.tensor_scalar(silu[:, :], csig[:, 1, :], 0.5, None, ALU.mult).then_inc(silu_ready, 1)

            def positions_sum(k):
                dve.wait_ge(xnat_in[k], 16)
                if k < 2:
                    src = hw(xnat)[:, :, 0:TB, :] if k == 0 else hw(xnat)[:, :, TB:, :]
                    link(dve.tensor_reduce(sums[:, 2 * k:2 * k + 2, :], src.rearrange("p s l d -> p s d l"), AX, ALU.add))
                else:
                    link(dve.tensor_reduce(sums[:, 4, :], xnat[:, 2 * LH:, :].rearrange("p l d -> p d l"), AX, ALU.add))

            def gate_sums():
                link(tt(sums[:, 0:2, :], sums[:, 0:2, :], sums[:, 2:4, :], ALU.add))
                tt(agg[:, 1:3, :], sums[:, 0:2, :], sums[:, 4, :].unsqueeze(1).to_broadcast([P, 2, P]),
                   ALU.add).then_inc(agg_ready, 1)
                dve.wait_ge(agg_ready, 1)
                tt(agg[:, 0, :], agg[:, 1, :], sums[:, 1, :], ALU.add).then_inc(agg_ready, 1)

            def gate_means():
                dve.wait_ge(agg_turned, 1)
                dve.tensor_scalar(aggT[:, 0, :], m[:, 1, 0:P], 1.0 / L, None, ALU.mult).then_inc(aggT_ready, 1)
                dve.tensor_scalar(aggT[:, 1:3, :], m[:, 1, P:3 * P].rearrange("p (a d) -> p a d", a=2),
                                  1.0 / (LH + LP), None, ALU.mult).then_inc(aggT_ready, 1)

            def gate_shift():
                dve.wait_ge(logits0, 1)
                link(dve.scalar_tensor_tensor(out=g0[:, 0, :], in0=rows[:, 0:E0], scalar=1.0, in1=m[:, 1, 408:412],
                                              op0=ALU.add, op1=ALU.mult))
                tt(g0[:, 1, :], g0[:, 0, :], rows[:, E0:2 * E0], ALU.add).then_inc(shifted0, 1)
                dve.wait_ge(shifted0, 1)
                dve.tensor_reduce(g0s[:, 0:1], g0[:, 1, :], AX, ALU.max, negate=True).then_inc(shifted0, 1)

            def find_best(values, found):
                best, scratch = g0s[:, 3:4], g0[:, 4, :]
                link(dve.tensor_reduce(best, values, AX, ALU.max))
                link(dve.scalar_tensor_tensor(out=scratch, in0=values, scalar=best, in1=order[:, E1 - E0:],
                                              op0=ALU.is_equal, op1=ALU.mult))
                link(dve.tensor_reduce(best, scratch, AX, ALU.max))
                link(dve.tensor_scalar(found, scratch, best, None, ALU.is_equal))

            def gate_weights(step):
                if step == 0:
                    dve.wait_ge(exp0, 1)
                    link(dve.reciprocal(g0s[:, 2:3], g0s[:, 1:2]))
                    link(dve.tensor_scalar(g0[:, 3, :], g0[:, 2, :], g0s[:, 2:3], None, ALU.mult))
                    find_best(g0[:, 3, :], g0[:, 5, :])
                    link(dve.scalar_tensor_tensor(out=g0[:, 6, :], in0=g0[:, 5, :], scalar=-BIG, in1=g0[:, 3, :],
                                                  op0=ALU.mult, op1=ALU.add))
                if step == 1:
                    find_best(g0[:, 6, :], g0[:, 7, :])
                    link(tt(g0[:, 4, :], g0[:, 5, :], g0[:, 7, :], ALU.add))
                    link(tt(g0[:, 5, :], g0[:, 4, :], g0[:, 3, :], ALU.mult))
                    link(dve.tensor_reduce(g0s[:, 4:5], g0[:, 5, :], AX, ALU.add))
                    link(dve.tensor_scalar(g0s[:, 5:6], g0s[:, 4:5], 1e-8, None, ALU.add))
                    link(dve.reciprocal(g0s[:, 4:5], g0s[:, 5:6]))
                    dve.tensor_scalar(wbe[:, :], g0[:, 5, :], g0s[:, 4:5], None, ALU.mult).then_inc(wbe_ready, 1)

            def spread_l0():
                dve.wait_ge(w_turned, 1)
                link(dve.tensor_copy(wT[:, :], m[0:E0, 1, 0:P]))
                tt(wdiag[:, :, :], wT[:, :].unsqueeze(1).to_broadcast([E0, E0, P]),
                   ident[0:E0, 0:E0].unsqueeze(2).to_broadcast([E0, E0, P]), ALU.mult).then_inc(wd_ready, 1)
                tt(wmask[:, :, :], wT[:, :].unsqueeze(1).to_broadcast([E0, 3, P]),
                   mask3[:, :].unsqueeze(2).to_broadcast([E0, 3, P]), ALU.mult).then_inc(wd_ready, 1)
                dve.wait_ge(wb_mm, 1)
                dve.tensor_copy(wb[:, :, :], m[:, 1, :].rearrange("p (e b) -> p e b", e=E0)).then_inc(wb_ready, 1)
                dve.wait_ge(wb_mm, 2)
                dve.tensor_scalar(base[:, :, :], m[:, 0, 0:3 * P].rearrange("p (k b) -> p k b", k=3),
                                  bT[:, 20:21], None, ALU.add).then_inc(wb_ready, 1)

            def first_hooks(p):
                if p == 0:
                    positions_sum(2)
                    gate_sums()
                    dve.wait_ge(rows_mm, 1)
                    dve.tensor_copy(rows[:, :], m[:, 1, 384:408]).then_inc(rows_ready, 1)
                if p == 2:
                    gate_means()
                if p == 3:
                    gate_shift()
                if p == 4:
                    gate_weights(0)
                if p == 5:
                    gate_weights(1)
                if p == 6:
                    dve.tensor_copy(rsplit[:, 0, :], rw[:, 0, :]).then_inc(r_ready, 1)
                    dve.wait_ge(r_ready, 1)
                    tt(rsplit[:, 1, :], rw[:, 0, :], rsplit[:, 0, :].bitcast(F32), ALU.subtract).then_inc(r_ready, 1)
                if p == 7:
                    spread_l0()

            def logits_l1(t0, t1, number):
                t = t1 - t0
                bank = m[:, 1, :] if number == 1 else y[:, 1, :]
                parts = bank[:, 0:t * 2 * E1].rearrange("p (t k e) -> p t k e", k=2, e=E1)
                value, work = g1[:, 0, t0:t1, :], g1[:, 2, t0:t1, :]
                dve.wait_ge(logits1, number)
                link(tt(work, parts[:, :, 0, :], rows[:, 8:16].unsqueeze(1).to_broadcast([P, t, E1]), ALU.add))
                tt(value, work, parts[:, :, 1, :], ALU.add).then_inc(logits1_ready if number == 1 else bank_read, 1)

            def choose_l1(step, t0, t1, number):
                t = t1 - t0
                value, score, work, chosen, second = (g1[:, k, t0:t1, :] for k in range(5))
                best, denom, inverse, over, half = (g1s[:, k, t0:t1] for k in range(5))

                def wide(v):
                    return v.unsqueeze(2).to_broadcast([P, t, E1])

                found = chosen if step < 4 else second
                if step == 0:
                    dve.wait_ge(exp1, number)
                    link(dve.tensor_scalar(work, score, 1.0, None, ALU.add))
                    link(dve.reciprocal(score, work))
                if step == 1:
                    link(tt(value, score, rows[:, 16:24].unsqueeze(1).to_broadcast([P, t, E1]), ALU.add))
                if step == 4:
                    link(dve.scalar_tensor_tensor(out=value, in0=chosen, scalar=-BIG, in1=value,
                                                  op0=ALU.mult, op1=ALU.add))
                if step in (1, 4):
                    link(dve.tensor_reduce(best, value, AX, ALU.max))
                if step in (2, 5):
                    link(tt(work, value, wide(best), ALU.is_equal))
                    link(tt(work, work, order[:, :].unsqueeze(1).to_broadcast([P, t, E1]), ALU.mult))
                if step in (3, 6):
                    link(dve.tensor_reduce(best, work, AX, ALU.max))
                    link(tt(found, work, wide(best), ALU.is_equal))
                if step == 7:
                    link(tt(chosen, chosen, second, ALU.add))
                    link(tt(work, chosen, score, ALU.mult))
                if step == 8:
                    link(dve.tensor_reduce(denom, work, AX, ALU.add))
                    link(dve.tensor_scalar(over, denom, 1e-9, None, ALU.is_gt))
                    link(dve.tensor_scalar(half, denom, 1e-9, None, ALU.add))
                if step == 9:
                    link(dve.reciprocal(inverse, half))
                    link(tt(inverse, inverse, over, ALU.mult))
                    dve.tensor_scalar(half, over, -0.5, 0.5, ALU.mult, ALU.add).then_inc(gates_scaled, 1)

            def sixth_hooks(p):
                if p == 3:
                    logits_l1(0, EARLY, 1)
                if p >= 5:
                    choose_l1(p - 5, 0, EARLY, 1)

            def last_hooks(p):
                if p < 5:
                    choose_l1(p + 5, 0, EARLY, 1)

            def gate_routed(b, p, between=None):
                buf = p % 2
                dve.wait_ge(gb_ready, b.routed + (p - 1))
                dve.wait_ge(h_ready, b.pairs + (p + 1))
                for j in range(2):
                    tt(h[:, buf, j, :], h[:, buf, j, :], m[:, j, :], ALU.mult).then_inc(gated, 1)
                if between:
                    between(p)
                for j in range(2):
                    dve.wait_ge(ghi_done, b.chunks + (2 * (p - 2) + j + 1))
                    last = tt(hlo[:, buf, j, :], h[:, buf, j, :], hhi[:, buf, j, :].bitcast(F32), ALU.subtract)
                last.then_inc(split_done, 1)

            def gate_shared(b):
                for p in range(C1):
                    dve.wait_ge(h_ready, b.pairs + (p + 1))
                    dve.wait_ge(z_ready, b.pairs * 2 + (2 * p + 2))
                    dve.scalar_tensor_tensor(out=h[:, p, 1, :], in0=h[:, p, 0, :], scalar=1.0, in1=z[:, 2 * p, :],
                                             op0=ALU.add, op1=ALU.mult).then_inc(half_gated, 1)
                    dve.wait_ge(half_gated, b.shared + (p + 1))
                    dve.scalar_tensor_tensor(out=h[:, p, 0, :], in0=h[:, p, 1, :], scalar=0.5,
                                             in1=z[:, 2 * p + 1, :], op0=ALU.mult, op1=ALU.mult).then_inc(swiglu, 1)
                if not b.first:
                    close_l1(b.pairs, b.index, b.shifted(-1))
                for p in range(C1):
                    dve.wait_ge(shared_hi, b.shared + (p + 1))
                    tt(hlo[:, p, 0, :], h[:, p, 0, :], hhi[:, p, 0, :].bitcast(F32),
                       ALU.subtract).then_inc(split_done, 1)

            def close_l1(pairs, number, columns):
                dve.wait_ge(mm2_done, pairs)
                if not (isinstance(number, int) and number == 1):
                    dve.wait_ge(bank_read, number)
                dve.scalar_tensor_tensor(out=x2T, in0=y[:, 0, :], scalar=1.0 / 3.0, in1=xT[:, columns],
                                         op0=ALU.mult, op1=ALU.add).then_inc(y_used, 1)

            def l1_block(b, between=None):
                gate_shared(b)
                if between:
                    between(0)
                for p in range(C1, L1_PAIRS):
                    gate_routed(b, p, between)

            last_l0 = Block("proprio", NB - 1)

            def first_l1(p):
                if p == 0:
                    job_out(last_l0, len(JOBS["proprio"]) - 1, last_l0.columns)
                if p == 3:
                    close_l0(last_l0, steps=(0,))
                if p == 4:
                    close_l0(last_l0, steps=(1,))

            def second_l1(p):
                if p == 0:
                    logits_l1(EARLY, L, 2)

            def choose_last(p, of):
                for step in {(2, 2): (0, 1), (2, 3): (2, 3), (2, 4): (4, 5), (2, 5): (6, 7), (3, 2): (8, 9)}.get((of, p), ()):
                    choose_l1(step, EARLY, L, 2)

            cond_prepare()
            positions_sum(0)
            x_copy(slice(0, BW), 1)
            dve.wait_ge(c_turned, 1)
            dve.tensor_copy(cT[:, :, :], m[:, 1, 0:2 * P].rearrange("p (a d) -> p a d", a=2)).then_inc(c_ready, 1)
            dve.wait_ge(xT_done, 1)
            dve.wait_ge(xhi_done, 1)
            tt(xlo[:, 0:BW], xT[:, 0:BW], xhi[:, 0:BW].bitcast(F32), ALU.subtract).then_inc(x_ready, 1)
            dve.wait_ge(bT_turned, 1)
            dve.tensor_copy(bT[:, :], y[:, 0, 0:21]).then_inc(bT_ready, 1)
            positions_sum(1)
            l0_block(Block("mixed", 0, first=True), None, True, first_hooks)
            with dve.Fori(0, NBM - 1) as r:
                l0_block(Block("mixed", 1, r), Block("mixed", 0, r), True)
            l0_block(Block("proprio", NBM), Block("mixed", NBM - 1), True)
            l0_block(Block("proprio", NBM + 1), Block("proprio", NBM), True, sixth_hooks)
            l0_block(Block("proprio", NB - 1), Block("proprio", NB - 2), False, last_hooks)
            l1_block(Block("l1", 0, first=True), first_l1)
            l1_block(Block("l1", 1), second_l1)
            l1_block(Block("l1", 2), lambda p: choose_last(p, 2))
            l1_block(Block("l1", 3), lambda p: choose_last(p, 3))
            with dve.Fori(0, NB - 4) as r:
                l1_block(Block("l1", 4, r))
            close_l1(L0_PAIRS + L1_PAIRS * NB, NB, slice((NB - 1) * BW, NB * BW))


_L0 = ["gate_w", "gate_b", "time_w", "time_b", "ew1", "eb1", "ew2", "eb2", "sw1", "sb1", "sw2", "sb2"]
_L1 = ["router_W", "router_bias", "w1", "w3", "w2", "W1e", "W2e"]
_INS = ["x", "cond_1024"] + ["L0_cond_" + n for n in _L0] + ["L1_cond_" + n for n in _L1]
_OUTS = [((P, L, P), "float32")]


def kernel(**inputs):
    import numpy as _np
    import concourse.bacc as _bacc
    from concourse import mybir as _mybir
    from concourse.bass_utils import run_bass_kernel_spmd as _run

    nc = _bacc.Bacc("TRN2", target_bir_lowering=False, num_devices=1)
    arrays, args = {}, []
    for name in _INS:
        a = _np.ascontiguousarray(inputs[name])
        arrays[f"in_{name}_dram"] = a
        args.append(nc.dram_tensor(f"in_{name}_dram", a.shape, _mybir.dt.from_np(a.dtype), kind="ExternalInput").ap())
    for i, (shape, dtype) in enumerate(_OUTS):
        dt = _mybir.dt.from_np(_np.dtype(dtype))
        args.append(nc.dram_tensor(f"out_{i}_dram", shape, dt, kind="ExternalOutput").ap())
    build(nc, *args)
    r = _run(nc, [arrays], core_ids=[0])
    return r.results[0]["out_0_dram"]
```

```python
from contextlib import ExitStack

import concourse.bass as bass
from concourse import mybir

ALU = mybir.AluOpType
ACT = mybir.ActivationFunctionType
AX = mybir.AxisListType.X
F32 = mybir.dt.float32
F32R = mybir.dt.float32r

P = 128
L = 32
LH = L // 3
LP = L - 2 * LH
E0, H0 = 4, 512
C0 = H0 // P
SH = E0
E1, HS1 = 8, 256
C1 = HS1 // P
TB = 4
BW = TB * P
HW = BW // 2
NB = L // TB
NBM = 2 * LH // TB
NBP = NB - NBM
BIG = 3.0e38

WHOLE = {e: [(e, 0, BW)] for e in (0, 1, 2, 3, SH)}
BOTH = [(1, 0, HW), (2, HW, BW)]
JOBS = {"mixed": [WHOLE[SH], WHOLE[0], WHOLE[3], BOTH],
        "proprio": [WHOLE[SH], WHOLE[0], WHOLE[1], WHOLE[2], WHOLE[3]]}
L0_PAIRS = 2 * (NBM * 4 + NBP * 5)
RUN = 2 * TB
RUNS = L // RUN
LATE_TURN = 3
PEELED = LATE_TURN + 1
EARLY = L - RUN
L0_PARTS = NBM * 3 + NBP * 4
L1_PAIRS = C1 + E1 // 2

O_W1, O_W3, O_W2 = 0, HS1, 2 * HS1
O_W1E = O_W2 + C1 * P
O_W2E = O_W1E + E1 * P
N_L1W = O_W2E + E1 * P
L1_PIECES = ((0, O_W1E), (O_W1E, O_W2E), (O_W2E, N_L1W))


W_ORDER = ((SH, 1), (0, 1), (SH, 2), (0, 2), (3, 0), (1, 0), (2, 0))
W_COLUMNS = {0: slice(0, 2 * H0), 1: slice(0, H0), 2: slice(H0, 2 * H0)}


class Block:

    def __init__(self, kind, start, step=0, first=False, of_parity=None):
        self.kind, self.first, self.parity = kind, first, start % 2
        self.of_parity = start // 2 if of_parity is None else of_parity
        self.index = step + start
        if kind == "mixed":
            self.pairs = step * 8 + 8 * start
            self.halves = step * 4 + 4 * start
            self.adds = step * 3 + 3 * start
        elif kind == "proprio":
            past = start - NBM
            self.pairs = step * 10 + (8 * NBM + 10 * past)
            self.halves = step * 5 + (4 * NBM + 5 * past)
            self.adds = step * 4 + (3 * NBM + 4 * past)
        else:
            self.pairs = step * L1_PAIRS + (L0_PAIRS + L1_PAIRS * start)
            self.shared = step * C1 + C1 * start
            self.routed = step * 4 + 4 * start
            self.chunks = step * E1 + E1 * start
        self.at = step * BW + start * BW
        self.columns = slice(self.at, self.at + BW) if isinstance(step, int) else bass.ds(self.at, BW)

    def shifted(self, by):
        at = self.at + by * BW
        return slice(at, at + BW) if isinstance(self.at, int) else bass.ds(at, BW)


def l0_last_adds(kind):
    return len(JOBS[kind]) - 1


def build(nc, x, cond, gate_w, gate_b, time_w, time_b, ew1, eb1, ew2, eb2, sw1, sb1, sw2, sb2,
          router_W, router_bias, w1, w3, w2, W1e, W2e, out):
    ctx = ExitStack()
    with ctx:
        def sb(name, shape, dt=F32):
            return ctx.enter_context(nc.sbuf_tensor("sb_" + name, shape, dt))

        def sem(name):
            return ctx.enter_context(nc.semaphore(name))

        z = ctx.enter_context(nc.psum_tensor("ps_z", [P, 4, BW], F32))
        y = ctx.enter_context(nc.psum_tensor("ps_y", [P, 2, BW], F32))
        m = ctx.enter_context(nc.psum_tensor("ps_m", [P, 2, BW], F32))
        
        xnat = sb("xnat", [P, L, P])
        xstage = sb("xstage", [P, TB, P])
        xT = sb("xT", [P, L * P])
        xhi, xlo = sb("xhi", [P, L * P], F32R), sb("xlo", [P, L * P], F32R)
        raw = sb("raw", [P, E0 + 1, 2 * H0])
        whi, wlo = sb("whi", [P, E0 + 1, 2 * H0], F32R), sb("wlo", [P, E0 + 1, 2 * H0], F32R)
        raw1 = raw[:, :, :].rearrange("p e n -> p (e n)")[:, 0:N_L1W]
        vhi, vlo = sb("vhi", [P, N_L1W], F32R), sb("vlo", [P, N_L1W], F32R)
        h = sb("h", [P, 2, 2, BW])
        hhi, hlo = sb("hhi", [P, 2, 2, BW], F32R), sb("hlo", [P, 2, 2, BW], F32R)
        acc = sb("acc", [P, BW])
        part = sb("part", [P, 2, BW])
        ident = sb("ident", [P, P])
        ones = sb("ones", [E0, P])
        mask3 = sb("mask3", [E0, 3])
        order = sb("order", [P, E1])
        brow = sb("brow", [21, P])
        bT = sb("bT", [P, 21])
        e2row = sb("e2row", [E0, P])
        vrow = sb("vrow", [1, 20])
        gw = sb("gw", [P, 3, E0])
        tw = sb("tw", [P, 2 * E0])
        rw = sb("rw", [P, 2, E1])
        rsplit = sb("rsplit", [P, 2, E1], F32R)
        cnat = sb("cnat", [P, P])
        csig = sb("csig", [P, 2, P])
        silu = sb("silu", [P, P])
        cT = sb("cT", [P, 2, P])
        gate_space = sb("gate_space", [P, 11, P])
        sums = gate_space[:, 0:5, :]
        agg, aggT = gate_space[:, 5:8, :], gate_space[:, 8:11, :]
        warm = sb("warm", [P, 2])
        rows = sb("rows", [P, 24])
        g0 = sb("g0", [P, 8, E0])
        g0s = sb("g0s", [P, 6])
        wbe = sb("wbe", [P, E0])
        wT = sb("wT", [E0, P])
        wdiag = sb("wdiag", [E0, E0, P])
        wmask = sb("wmask", [E0, 3, P])
        wb = sb("wb", [P, E0, P])
        base = sb("base", [P, 3, P])
        g1 = sb("g1", [P, 5, L, E1])
        g1s = sb("g1s", [P, 5, L])
        gates = sb("gates", [P, NB, E1, TB])
        gT = sb("gT", [RUN * E1, RUNS, P])
        raw_flat = raw[:, :, :].rearrange("p e n -> p (e n)")
        wide_gates = [xnat[:, :, :].rearrange("p l d -> p (l d)"), raw_flat[:, 0:E1 * BW]]
        x2T = raw_flat[:, E1 * BW:(E1 + 1) * BW]
        ostage = raw_flat[:, (E1 + 1) * BW:(E1 + 2) * BW].rearrange("p (t d) -> p t d", t=TB)
        third = gate_space[:, :, :].rearrange("p n s -> p (n s)")[:, 0:2 * BW].rearrange("p (j n) -> p j n", j=2)
        h1 = [h[:, 0, :, :], h[:, 1, :, :], third]
        gates_row = nc.dram_tensor("gates_row", [NB, E1 * BW], F32, kind="Internal").ap()

        x_in, rows_in, gates_in = sem("x_in"), sem("rows_in"), sem("gates_in")
        xnat_in = [sem(f"xnat_in{k}") for k in range(3)]
        c_in, b_in, e2_in = sem("c_in"), sem("b_in"), sem("e2_in")
        w_in = [[sem(f"w{k}_in{e}") for k in (1, 2)] for e in range(E0 + 1)]
        v_in = sem("v_in")
        consts, warm_ready = sem("consts"), sem("warm_ready")
        x_turned = sem("x_turned")
        xhi_done, xT_done = sem("xhi_done"), sem("xT_done")
        x_ready = sem("x_ready")
        w_hi_done = sem("w_hi_done")
        w_ready = sem("w_ready")
        v_hi_done, v_ready = sem("v_hi_done"), sem("v_ready")
        r_ready = sem("r_ready")
        z_ready = sem("z_ready")
        h_ready = sem("h_ready")
        hi_act, hi_dve = sem("hi_act"), sem("hi_dve")
        split_done = sem("split_done")
        second_split = sem("second_split")
        mm2_done = sem("mm2_done")
        part_ready = sem("part_ready")
        y_used = sem("y_used")
        part_weighted = sem("part_weighted")
        base_added = sem("base_added")
        adds_done = sem("adds_done")
        x1hi_done, x1_ready = sem("x1hi_done"), sem("x1_ready")
        half_gated, swiglu = sem("half_gated"), sem("swiglu")
        shared_hi = sem("shared_hi")
        row_written = sem("row_written")
        wide_in = [sem("wide_in_even"), sem("wide_in_odd")]
        gated = sem("gated")
        ghi_done = sem("ghi_done")
        out_turned, stored = sem("out_turned"), sem("stored")
        bank_read = sem("bank_read")
        bT_turned, bT_ready = sem("bT_turned"), sem("bT_ready")
        c_tanh, c_turned, rows_mm, rows_ready = sem("c_tanh"), sem("c_turned"), sem("rows_mm"), sem("rows_ready")
        c_ready = sem("c_ready")
        silu_ready = sem("silu_ready")
        agg_ready, agg_turned, aggT_ready = sem("agg_ready"), sem("agg_turned"), sem("aggT_ready")
        logits0, shifted0, exp0 = sem("logits0"), sem("shifted0"), sem("exp0")
        wbe_ready, w_turned, wd_ready = sem("wbe_ready"), sem("w_turned"), sem("wd_ready")
        wb_mm, wb_ready = sem("wb_mm"), sem("wb_ready")
        logits1, logits1_ready, exp1 = sem("logits1"), sem("logits1_ready"), sem("exp1")
        gates_scaled = sem("gates_scaled")
        gates_ready, g_turned, gT_ready = sem("gates_ready"), sem("g_turned"), sem("gT_ready")
        pool_step = sem("pool_step")
        dve_step = sem("dve_step")

        block = ctx.enter_context(nc.Block())

        def hw(tensor):
            return tensor[:, 0:2 * LH, :].rearrange("p (s l) d -> p s l d", s=2)

        def part_of(b, j):
            return x2T if b.first and j == 1 else part[:, j % 2, :]

        @block.sync
        def _(sp):
            def mixed(tensor, at):
                return hw(tensor)[:, :, bass.ds(at, TB // 2), :]

            def weights(e, layer):
                src = (sw1, sw2)[layer - 1] if e == SH else (ew1, ew2)[layer - 1][e]
                if layer == 2:
                    src = src.rearrange("(c h) d -> h c d", c=C0)
                sp.dma_start(raw[:, e, W_COLUMNS[layer]], src).then_inc(w_in[e][layer - 1], 16)

            sp.dma_start(hw(xnat)[:, :, 0:TB, :], hw(x)[:, :, 0:TB, :]).then_inc(xnat_in[0], 16)
            sp.dma_start(cnat[:, :], cond).then_inc(c_in, 16)
            weights(SH, 1)
            weights(SH, 2)
            weights(0, 1)
            sp.dma_start(hw(xnat)[:, :, TB:, :], hw(x)[:, :, TB:, :]).then_inc(xnat_in[1], 16)
            weights(0, 2)
            sp.dma_start(tw[:, :], time_w).then_inc(rows_in, 16)
            sp.dma_start(vrow[:, 4:12], time_b.rearrange("(a h) -> a h", a=1)).then_inc(rows_in, 16)
            sp.dma_start(rw[:, :, :], router_W.rearrange("(j p) e -> p j e", j=2)).then_inc(rows_in, 16)
            sp.dma_start(vrow[:, 12:20], router_bias.rearrange("(a h) -> a h", a=1)).then_inc(rows_in, 16)
            sp.dma_start(xnat[:, 2 * LH:, :], x[:, 2 * LH:, :]).then_inc(xnat_in[2], 16)
            sp.dma_start(gw[:, :, :], gate_w.rearrange("(j p) e -> p j e", j=3)).then_inc(gates_in, 16)
            sp.dma_start(vrow[:, 0:4], gate_b.rearrange("(a h) -> a h", a=1)).then_inc(gates_in, 16)
            for e in (3, 1, 2):
                weights(e, 1)
                weights(e, 2)
            staged = xstage[:, :, :].rearrange("p (s l) d -> p s l d", s=2)
            sp.dma_start(staged, mixed(x, TB)).then_inc(x_in, 16)
            sp.wait_ge(w_ready, len(W_ORDER))
            for at, n, src in ((O_W1, HS1, w1), (O_W3, HS1, w3),
                               (O_W2, C1 * P, w2.rearrange("(c h) d -> h c d", c=C1)),
                               (O_W1E, E1 * P, W1e.rearrange("e c h -> c e h")),
                               (O_W2E, E1 * P, W2e.rearrange("e h d -> h e d"))):
                sp.dma_start(raw1[:, at:at + n], src).then_inc(v_in, 16)
            with sp.Fori(0, NBM - 3) as r:
                sp.wait_ge(x_turned, r + 3)
                sp.dma_start(staged, mixed(x, r * 2 + 6)).then_inc(x_in, 16)
            with sp.Fori(0, NBP) as r:
                sp.wait_ge(x_turned, r + NBM)
                sp.dma_start(xstage[:, :, :], x[:, bass.ds(r * TB + 2 * LH, TB), :]).then_inc(x_in, 16)

            def write_gates(k0, k1, number):
                sp.wait_ge(gT_ready, number)
                rows = gates_row.rearrange("b (r s) -> (b r) s", s=P).rearrange("(k r) s -> r k s", k=RUNS)
                sp.dma_start(rows[:, k0:k1, :], gT[:, k0:k1, :]).then_inc(row_written, 16)
                sp.wait_ge(row_written, 16 * number)

            def spread_gates(n):
                row = gates_row[n:n + 1, :].to_broadcast([P, E1 * BW])
                sp.dma_start(wide_gates[n % 2], row).then_inc(wide_in[n % 2], 16)

            def store(n):
                sp.wait_ge(bank_read, n + 1)
                for half, at in ((0, n * 2), (2, n * 2 + LH)) if n < NBM else ((0, n * TB), (2, n * TB + 2)):
                    if n == NB - 1 and half:
                        sp.wait_ge(bank_read, NB + 1)
                    sp.dma_start(out[:, at:at + 2, :], ostage[:, half:half + 2, :]).then_inc(stored, 16)

            sp.wait_ge(v_ready, len(L1_PIECES))
            write_gates(0, RUNS - 1, 1)
            spread_gates(0)
            spread_gates(1)
            for n in range(NB):
                if n + 2 < NB:
                    sp.wait_ge(gated, E1 * (n + 1))
                    if n + 2 == EARLY // TB:
                        write_gates(RUNS - 1, RUNS, 2)
                    spread_gates(n + 2)
                store(n)
            sp.wait_ge(stored, 32 * NB)

        @block.gpsimd
        def _(pool):
            pool.memset(warm[:, 0:1], 0.0).then_inc(warm_ready, 1)
            pool.memset(ident[:, :], 0.0).then_inc(consts, 1)
            pool.memset(mask3[:, :], 1.0).then_inc(consts, 1)
            pool.memset(ones[:, :], 1.0).then_inc(consts, 1)
            for e in range(E1):
                pool.memset(order[:, e:e + 1], float(E1 - e)).then_inc(consts, 1)
            pool.wait_ge(consts, 3 + E1)

            def diagonal(tile):
                return pool.affine_select(out=tile[:, :], in_=tile[:, :], compare_op=ALU.not_equal, fill=1.0,
                                          base=0, pattern=[[-1, P]], channel_multiplier=1)

            diagonal(ident).then_inc(consts, 1)
            pool.affine_select(out=mask3[:, 0:2], in_=mask3[:, 0:2], compare_op=ALU.not_equal, fill=0.0,
                               base=-2, pattern=[[1, 2]], channel_multiplier=1).then_inc(consts, 1)
            for dst, src in ((brow[16:20, :], sb1.rearrange("(c h) -> c h", c=C0)),
                             (brow[0:16, :], eb1.rearrange("e (c h) -> (e c) h", c=C0)),
                             (brow[20:21, :], sb2.rearrange("(a h) -> a h", a=1))):
                pool.dma_start(dst, src).then_inc(b_in, 16)
            pool.dma_start(e2row[:, :], eb2).then_inc(e2_in, 16)

            def x_lo(b, columns, number):
                pool.wait_ge(xhi_done, number)
                pool.tensor_tensor(xlo[:, columns], xT[:, columns], xhi[:, columns].bitcast(F32),
                                   ALU.subtract).then_inc(x_ready, 1)

            def w_lo(n):
                e, columns = W_ORDER[n][0], W_COLUMNS[W_ORDER[n][1]]
                pool.wait_ge(w_hi_done, n + 1)
                pool.tensor_tensor(wlo[:, e, columns], raw[:, e, columns], whi[:, e, columns].bitcast(F32),
                                   ALU.subtract).then_inc(w_ready, 1)

            def v_lo(n):
                at, end = L1_PIECES[n]
                pool.wait_ge(v_hi_done, n + 1)
                pool.tensor_tensor(vlo[:, at:end], raw1[:, at:end], vhi[:, at:end].bitcast(F32),
                                   ALU.subtract).then_inc(v_ready, 1)

            def add_base(b):
                pool.wait_ge(y_used, b.index + 1)
                pool.wait_ge(wb_ready, 2)
                if b.first:
                    pool.wait_ge(adds_done, 2)
                if b.kind == "mixed":
                    other = base[:, 0:2, :].unsqueeze(2).to_broadcast([P, 2, 2, P])
                    own = acc[:, :].rearrange("p (a b c) -> p a b c", a=2, b=2)
                else:
                    other = base[:, 2, :].unsqueeze(1).to_broadcast([P, TB, P])
                    own = acc[:, :].rearrange("p (b c) -> p b c", b=TB)
                pool.tensor_tensor(own, own, other, ALU.add).then_inc(base_added, 1)

            def add_part(b, j):
                pool.wait_ge(part_ready, b.adds + j)
                if b.first:
                    pool.wait_ge(*((y_used, 1) if j == 1 else (adds_done, 1) if j == 2 else (base_added, 1)))
                elif j == 1:
                    pool.wait_ge(base_added, b.index + 1)
                else:
                    pool.wait_ge(adds_done, b.adds + (j - 1))
                pool.tensor_tensor(acc[:, :], acc[:, :], part_of(b, j), ALU.add).then_inc(adds_done, 1)

            def weight_part(b, j):
                pool.wait_ge(part_ready, j)
                pool.wait_ge(wb_ready, 1)
                own = part_of(b, j).rearrange("p (b c) -> p b c", b=TB)
                weights = wb[:, JOBS[b.kind][j][0][0], :].unsqueeze(1).to_broadcast([P, TB, P])
                pool.tensor_tensor(own, own, weights, ALU.mult).then_inc(part_weighted, 1)
                pool.wait_ge(part_weighted, j)

            def l0_block(b, next_x, hooks=None):
                if b.first:
                    x_lo(b, b.shifted(1), 2)
                    for j in (1, 2):
                        weight_part(b, j)
                        add_part(b, j)
                    add_base(b)
                    add_part(b, 3)
                    return
                for j in range(len(JOBS[b.kind])):
                    if j == 0:
                        add_base(b)
                    else:
                        add_part(b, j)
                    if j == 1 and next_x:
                        x_lo(b, b.shifted(1), b.index + 2)
                    if hooks:
                        hooks(j)

            steps = [0]

            def link(ins):
                steps[0] += 1
                ins.then_inc(pool_step, 1)
                pool.wait_ge(pool_step, steps[0])

            def finish_gates(n0, n1, number):
                at, shape = slice(n0 * TB, n1 * TB), [P, (n1 - n0) * TB, E1]
                work, chosen, low = (g1[:, k, at, :] for k in (2, 3, 4))
                inverse, half = (g1s[:, k, at].unsqueeze(2).to_broadcast(shape) for k in (2, 4))
                pool.wait_ge(gates_scaled, number)
                link(pool.tensor_tensor(work, work, inverse, ALU.mult))
                link(pool.tensor_tensor(low, chosen, half, ALU.mult))
                pool.tensor_tensor(gates[:, n0:n1, :, :].rearrange("p b e t -> p b t e"),
                                   work.rearrange("p (b t) e -> p b t e", t=TB),
                                   low.rearrange("p (b t) e -> p b t e", t=TB), ALU.add).then_inc(gates_ready, 1)

            for n in range(len(W_ORDER)):
                w_lo(n)
            l0_block(Block("mixed", 0, first=True), True)
            with pool.Fori(0, NBM - 1) as r:
                l0_block(Block("mixed", 1, r), True)
            l0_block(Block("proprio", NBM), True, lambda j: v_lo(j - 1) if 1 <= j <= 3 else None)
            l0_block(Block("proprio", NBM + 1), True)

            l0_block(Block("proprio", NB - 1), False, lambda j: finish_gates(0, EARLY // TB, 1) if j == 1 else None)

            def l1_block(b, hooks=None):
                for p in range(C1, L1_PAIRS):
                    pool.wait_ge(ghi_done, b.chunks + (2 * (p - 2) + 2))
                    pool.tensor_tensor(hlo[:, p % 2, 1, :], h1[p % 3][:, 1, :], hhi[:, p % 2, 1, :].bitcast(F32),
                                       ALU.subtract).then_inc(second_split, 1)
                    if hooks:
                        hooks(p)

            for k in range(LATE_TURN):
                l1_block(Block("l1", k))
            l1_block(Block("l1", LATE_TURN), lambda p: finish_gates(EARLY // TB, NB, 2) if p == 3 else None)
            with pool.Fori(0, NB - PEELED) as r:
                l1_block(Block("l1", PEELED, r))

        @block.scalar
        def _(act):
            def x_hi(columns, number):
                act.wait_ge(xT_done, number)
                act.activation(xhi[:, columns], xT[:, columns], ACT.Copy).then_inc(xhi_done, 1)

            def w_hi(n):
                e, layer = W_ORDER[n]
                for k in (1, 2) if layer == 0 else (layer,):
                    act.wait_ge(w_in[e][k - 1], 16)
                columns = W_COLUMNS[layer]
                act.activation(whi[:, e, columns], raw[:, e, columns], ACT.Copy).then_inc(w_hi_done, 1)

            def hidden_l0(b, p):
                buf = p % 2
                for j in range(2):
                    c = 2 * (p % 2) + j
                    act.wait_ge(z_ready, b.pairs * 2 + (2 * p + j + 1))
                    if j == 0 and not (b.first and p < 2):
                        act.wait_ge(split_done, b.pairs + (p - 1))
                    for e, lo, hi in JOBS[b.kind][p // 2]:
                        last = act.activation(h[:, buf, j, lo:hi], z[:, 2 * buf + j, lo:hi],
                                              ACT.Gelu_apprx_tanh, bias=bT[:, C0 * e + c:C0 * e + c + 1])
                last.then_inc(h_ready, 1)
                if p % 2 == 0:
                    act.wait_ge(h_ready, b.pairs + (p + 1))
                    if not (b.first and p < 2):
                        act.wait_ge(mm2_done, b.pairs + (p - 1))
                    act.activation(hhi[:, buf, :, :], h[:, buf, :, :], ACT.Copy).then_inc(hi_act, 1)

            def l0_block(b, next_x, hooks=None):
                for p in range(2 * len(JOBS[b.kind])):
                    hidden_l0(b, p)
                    if p == 4 and next_x:
                        x_hi(b.shifted(1), b.index + 2)
                    if hooks:
                        hooks(p)

            def first_hooks(p):
                if p < 4:
                    w_hi(p + 3)
                if p == 4:
                    act.wait_ge(shifted0, 2)
                    act.activation(g0[:, 2, :], g0[:, 1, :], ACT.Exp, bias=g0s[:, 0:1],
                                   accum_out=g0s[:, 1:2]).then_inc(exp0, 1)

            def fifth_hooks(p):
                if p < 3:
                    at, end = L1_PIECES[p]
                    act.wait_ge(v_in, 16 * 5)
                    act.activation(vhi[:, at:end], raw1[:, at:end], ACT.Copy).then_inc(v_hi_done, 1)

            def sixth_hooks(p):
                if p == 4:
                    exp_router(0, EARLY, 1)

            def last_hooks(p):
                if p == 9:
                    act.activation(warm[:, 1:2], warm[:, 0:1], ACT.Gelu)
                if p == 7:
                    turned_gates(0, RUNS - 1, 1)

            def exp_router(t0, t1, number):
                act.wait_ge(logits1_ready, number)
                act.activation(g1[:, 1, t0:t1, :], g1[:, 0, t0:t1, :], ACT.Exp, scale=-1.0).then_inc(exp1, 1)

            def gated_hi(b, p, before):
                for j in range(2):
                    n = b.chunks + (2 * (p - 2) + j + 1 - (E1 if before else 0))
                    act.wait_ge(gated, n)
                    if j == 0:
                        act.wait_ge(mm2_done, b.pairs + (p - 1 - (L1_PAIRS if before else 0)))
                    act.activation(hhi[:, p % 2, j, :], h1[p % 3][:, j, :], ACT.Copy).then_inc(ghi_done, 1)

            def copy_out(number):
                act.wait_ge(out_turned, number)
                if not (isinstance(number, int) and number == 1):
                    act.wait_ge(stored, (number - 1) * 32)
                act.activation(ostage, y[:, 1, :].rearrange("p (t d) -> p t d", t=TB),
                               ACT.Copy).then_inc(bank_read, 1)

            def shared_chunk_hi(b, p):
                act.wait_ge(swiglu, b.shared + (p + 1))
                act.wait_ge(mm2_done, b.pairs + (p - 1))
                act.activation(hhi[:, p, 0, :], h[:, p, 0, :], ACT.Copy).then_inc(shared_hi, 1)

            def l1_block(b, hooks=None):
                for p in range(L1_PAIRS):
                    buf = p % 2
                    act.wait_ge(split_done, b.pairs + (p - (1 if b.first and p < 2 else 2)))
                    if p == 5 or (p < 3 and not b.first):
                        act.wait_ge(second_split, b.routed + (p - 2 if p < 3 else 1))
                    if p < C1:
                        act.wait_ge(z_ready, b.pairs * 2 + (2 * p + 1))
                        act.activation(h1[p][:, 0, :], z[:, 2 * buf, :], ACT.Tanh, scale=0.5).then_inc(h_ready, 1)
                    else:
                        act.wait_ge(z_ready, b.pairs * 2 + (2 * p + 2))
                        act.activation(h1[p % 3], z[:, 2 * buf:2 * buf + 2, :], ACT.Gelu).then_inc(h_ready, 1)
                    if p == 0 and not b.first:
                        gated_hi(b, L1_PAIRS - 1, True)
                    if p > 2:
                        gated_hi(b, p - 1, False)
                    if p == 1:
                        shared_chunk_hi(b, 0)
                        shared_chunk_hi(b, 1)
                    if p == 3 and not b.first:
                        copy_out(b.index)
                    if hooks:
                        hooks(p)

            def turned_gates(k0, k1, number):
                act.wait_ge(g_turned, number)
                src = m[0:RUN * E1, 0, 0:(k1 - k0) * P].rearrange("p (k s) -> p k s", s=P)
                act.activation(gT[:, k0:k1, :], src, ACT.Copy).then_inc(gT_ready, 1)

            act.wait_ge(warm_ready, 1)
            act.activation(warm[:, 1:2], warm[:, 0:1], ACT.Gelu_apprx_tanh)
            act.wait_ge(c_in, 16)
            act.activation(csig[:, 0, :], cnat[:, :], ACT.Tanh, scale=0.5).then_inc(c_tanh, 1)
            w_hi(0)
            x_hi(slice(0, BW), 1)
            w_hi(1)
            w_hi(2)
            act.wait_ge(bT_ready, 1)
            l0_block(Block("mixed", 0, first=True), True, first_hooks)
            with act.Fori(0, NBM - 1) as r:
                l0_block(Block("mixed", 1, r), True)
            l0_block(Block("proprio", NBM), True, fifth_hooks)
            l0_block(Block("proprio", NBM + 1), True, sixth_hooks)
            l0_block(Block("proprio", NB - 1), False, last_hooks)

            def early_hooks(k):
                def hooks(p):
                    if p == 2 and k == LATE_TURN + 1:
                        turned_gates(RUNS - 1, RUNS, 2)
                    if k == 1 and p == 5:
                        exp_router(EARLY, L, 2)
                return hooks

            for k in range(PEELED + 1):
                l1_block(Block("l1", k, first=k == 0), early_hooks(k))
            with act.Fori(0, NB - PEELED - 1) as r:
                l1_block(Block("l1", PEELED + 1, r))
            gated_hi(Block("l1", NB), L1_PAIRS - 1, True)
            act.wait_ge(stored, (NB - 1) * 32)
            for k, bank in enumerate((y[:, 1, :], m[:, 0, :])):
                act.wait_ge(out_turned, NB + k)
                act.activation(ostage[:, 2 * k:2 * k + 2, :], bank[:, 0:HW].rearrange("p (t d) -> p t d", t=2),
                               ACT.Copy).then_inc(bank_read, 1)

        @block.tensor
        def _(pe):
            def three(dst, hi, lo, rhs_hi, rhs_lo, start, stop, **kw):
                pe.matmul(dst, hi, rhs_hi, start=start, stop=False, **kw)
                pe.matmul(dst, lo, rhs_hi, start=False, stop=False, **kw)
                return pe.matmul(dst, hi, rhs_lo, start=False, stop=stop, **kw)

            def turn_x(number, positions=None):
                if positions is None:
                    pe.wait_ge(wb_ready, 2)
                    pe.wait_ge(x_in, number * 16 - 32)
                    pe.wait_ge(xT_done, number - 1)
                for t in range(TB):
                    src = xstage[:, t, :] if positions is None else xnat[:, positions[t], :]
                    last = pe.transpose(m[:, 0, t * P:(t + 1) * P], src, ident[:, :])
                last.then_inc(x_turned, 1)

            def first_layer_l0(b, p, by=0):
                buf = p % 2
                if not (b.first and p < 2 and not by):
                    pe.wait_ge(h_ready, b.pairs + (p - 1))
                if p == 0:
                    pe.wait_ge(x_ready, b.index + 1)
                for j in range(2):
                    c = 2 * (p % 2) + j
                    for e, lo, hi in JOBS[b.kind][p // 2]:
                        cols = bass.ds(b.at + lo, hi - lo)
                        last = three(z[:, 2 * buf + j, lo:hi], whi[:, e, c * P:(c + 1) * P],
                                     wlo[:, e, c * P:(c + 1) * P], xhi[:, cols], xlo[:, cols], True, True)
                    last.then_inc(z_ready, 1)

            def second_layer_l0(b, p):
                n_jobs = len(JOBS[b.kind])
                j0, buf = p // 2, p % 2
                bank = (n_jobs - 1 - j0) % 2
                pe.wait_ge(split_done, b.pairs + (p + 1))
                if p % 2 == 0:
                    if j0 == 2:
                        pe.wait_ge(y_used, b.index + 1)
                    elif j0 > 2:
                        pe.wait_ge(part_ready, b.adds + (j0 - 2))
                    elif not b.first:
                        pe.wait_ge(part_ready, b.adds)
                segments = JOBS[b.kind][j0]
                for j in range(2):
                    c = 2 * (p % 2) + j
                    for n, (e, lo, hi) in enumerate(segments):
                        at = H0 + c * P
                        last = three(y[:, bank, lo:hi], whi[:, e, at:at + P], wlo[:, e, at:at + P],
                                     hhi[:, buf, j, lo:hi], hlo[:, buf, j, lo:hi],
                                     c == 0 and n == 0, c == C0 - 1, skip_group_check=len(segments) > 1)
                last.then_inc(mm2_done, 1)

            def l0_block(b, following, next_x, hooks=None):
                n = 2 * len(JOBS[b.kind])
                for p in range(n):
                    if b.first and p % 2 == 0 and p + 2 < n:
                        pe.wait_ge(w_ready, {0: 2, 2: 5, 4: 7}[p])
                    if p + 2 < n:
                        first_layer_l0(b, p + 2)
                    else:
                        following(p + 2 - n)
                    if b.first and p in (0, 2):
                        pe.wait_ge(w_ready, 3 if p == 0 else 4)
                    second_layer_l0(b, p)
                    if p == 1 and b.first:
                        pe.wait_ge(xT_done, 1)
                        turn_x(2, (2, 3, LH + 2, LH + 3))
                    elif p == 1 and next_x:
                        turn_x(b.index + 2)
                    if hooks:
                        hooks(p)

            def turn_cond():
                pe.wait_ge(silu_ready, 1)
                pe.transpose(m[:, 1, 0:P], silu[:, :], ident[:, :])
                pe.transpose(m[:, 1, P:2 * P], cnat[:, :], ident[:, :]).then_inc(c_turned, 1)

            def gate_rows():
                pe.wait_ge(rows_in, 16 * 4)
                pe.wait_ge(c_ready, 1)
                pe.matmul(m[:, 1, 384:392], cT[:, 0, :], tw[:, :], start=True, stop=False)
                pe.matmul(m[:, 1, 384:392], ones[0:1, :], vrow[:, 4:12], start=False, stop=True)
                pe.matmul(m[:, 1, 392:400], cT[:, 1, :], rw[:, 1, :], start=True, stop=True)
                pe.matmul(m[:, 1, 400:408], ones[0:1, :], vrow[:, 12:20], start=True, stop=True).then_inc(rows_mm, 1)

            def gate_means():
                pe.wait_ge(rows_ready, 1)
                pe.wait_ge(agg_ready, 2)
                for j in range(3):
                    last = pe.transpose(m[:, 1, j * P:(j + 1) * P], agg[:, j, :], ident[:, :])
                last.then_inc(agg_turned, 1)

            def gate_logits():
                pe.wait_ge(gates_in, 16 * 2)
                pe.wait_ge(aggT_ready, 2)
                for j in range(3):
                    pe.matmul(m[:, 1, 408:412], aggT[:, j, :], gw[:, j, :], start=j == 0, stop=False)
                pe.matmul(m[:, 1, 408:412], ones[0:1, :], vrow[:, 0:4], start=False, stop=True).then_inc(logits0, 1)

            def first_hooks(p):
                if p == 0:
                    gate_rows()
                if p == 1:
                    gate_means()
                if p == 2:
                    gate_logits()
                if p == 6:
                    pe.wait_ge(wbe_ready, 1)
                    pe.matmul(m[0:E0, 1, 0:P], wbe[:, :], ident[:, :], start=True, stop=True).then_inc(w_turned, 1)
                if p == 7:
                    pe.wait_ge(wd_ready, 2)
                    pe.matmul(m[:, 1, :], ones[:, :], wdiag[:, :, :].rearrange("k e b -> k (e b)"),
                              start=True, stop=True).then_inc(wb_mm, 1)
                    pe.wait_ge(xT_done, 2)
                    pe.wait_ge(e2_in, 16)
                    pe.matmul(m[:, 0, 0:3 * P], e2row[:, :], wmask[:, :, :].rearrange("k e b -> k (e b)"),
                              start=True, stop=True).then_inc(wb_mm, 1)

            def route(block, dst, first):
                pe.wait_ge(x1_ready, 2 * (block + 1))
                for t in range(block * TB, (block + 1) * TB):
                    at = slice(t * P, (t + 1) * P)
                    to = (t - first) * 2 * E1
                    pe.matmul(dst[:, to:to + 2 * E1], xhi[:, at], rsplit[:, :, :].rearrange("p k e -> p (k e)"),
                              start=True, stop=False, skip_group_check=True)
                    last = pe.matmul(dst[:, to:to + E1], xlo[:, at], rsplit[:, 0, :],
                                     start=False, stop=True, skip_group_check=True)
                return last

            def turn_gates(k0, k1, number):
                pe.wait_ge(gates_ready, number)
                for k in range(k0, k1):
                    last = pe.transpose(m[0:RUN * E1, 0, (k - k0) * P:(k - k0 + 1) * P],
                                        gates[:, 2 * k:2 * k + 2, :, :].rearrange("p b e t -> p (b e t)"), ident[:, :])
                last.then_inc(g_turned, 1)

            def fifth_hooks(p):
                if p == 2:
                    pe.wait_ge(r_ready, 2)
                if 2 <= p < 2 + NBM:
                    route(p - 2, m[:, 1, :], 0)

            def sixth_hooks(p):
                if p == 2:
                    route(NBM, m[:, 1, :], 0).then_inc(logits1, 1)

            def last_hooks(p):
                if p == 6:
                    pe.wait_ge(xT_done, NB)
                    turn_gates(0, RUNS - 1, 1)

            def first_layer_l1(b, p):
                buf = p % 2
                if p in (2, 3):
                    pe.wait_ge(swiglu, b.shared + (p - 1))
                else:
                    pe.wait_ge(h_ready, b.pairs + (p - 1))
                if b.first and p in (0, 2):
                    pe.wait_ge(v_ready, 1 if p == 0 else 2)
                if p < 2:
                    offsets = (O_W1 + p * P, O_W3 + p * P)
                else:
                    offsets = tuple(O_W1E + (2 * (p - 2) + j) * P for j in range(2))
                for j, at in enumerate(offsets):
                    three(z[:, 2 * buf + j, :], vhi[:, at:at + P], vlo[:, at:at + P],
                          xhi[:, b.columns], xlo[:, b.columns], True, True).then_inc(z_ready, 1)

            def second_layer_l1(b, p):
                buf = p % 2
                if p == 2 and b.first:
                    pe.wait_ge(v_ready, 3)
                if p == 0 and b.first:
                    pe.wait_ge(part_ready, L0_PARTS)
                elif p == 0:
                    pe.wait_ge(y_used, b.index + NB)
                if p < 2:
                    pe.wait_ge(split_done, b.pairs + (p + 1))
                    at = O_W2 + p * P
                    last = three(y[:, 0, :], vhi[:, at:at + P], vlo[:, at:at + P],
                                 hhi[:, buf, 0, :], hlo[:, buf, 0, :], p == 0, False)
                else:
                    at = [O_W2E + (2 * (p - 2) + j) * P for j in range(2)]
                    for j in range(2):
                        pe.wait_ge(ghi_done, b.chunks + (2 * (p - 2) + j + 1))
                        for weights in (vhi, vlo):
                            pe.matmul(y[:, 0, :], weights[:, at[j]:at[j] + P], hhi[:, buf, j, :],
                                      start=False, stop=False)
                    pe.wait_ge(split_done, b.pairs + (p + 1))
                    pe.matmul(y[:, 0, :], vhi[:, at[0]:at[0] + P], hlo[:, buf, 0, :], start=False, stop=False)
                    pe.wait_ge(second_split, b.routed + (p - 1))
                    last = pe.matmul(y[:, 0, :], vhi[:, at[1]:at[1] + P], hlo[:, buf, 1, :],
                                     start=False, stop=p == L1_PAIRS - 1)
                last.then_inc(mm2_done, 1)

            def turn_out(number):
                pe.wait_ge(y_used, number + NB)
                if not (isinstance(number, int) and number == 1):
                    pe.wait_ge(bank_read, number - 1)
                for t in range(TB):
                    last = pe.transpose(y[:, 1, t * P:(t + 1) * P], x2T[:, t * P:(t + 1) * P], ident[:, :])
                last.then_inc(out_turned, 1)

            def l1_block(b, following=None, hooks=None):
                for p in range(L1_PAIRS):
                    if p + 2 < L1_PAIRS:
                        first_layer_l1(b, p + 2)
                    elif following:
                        following(p + 2 - L1_PAIRS)
                    if p == 1:
                        second_layer_l1(b, 0)
                    if p > 0:
                        second_layer_l1(b, p)
                    if p == 1 and not b.first:
                        turn_out(b.index)
                    if hooks:
                        hooks(p)

            def keep_busy(n):
                for _ in range(n):
                    pe.matmul(z[:, 3, 0:P], ident[:, :], ident[:, :], start=True, stop=True)

            b = Block("mixed", 0, first=True)
            pe.wait_ge(consts, 5 + E1)
            keep_busy(4)
            pe.wait_ge(xnat_in[0], 16)
            turn_x(1, (0, 1, LH, LH + 1))
            turn_cond()
            keep_busy(4)
            pe.wait_ge(w_ready, 1)
            first_layer_l0(b, 0)
            pe.wait_ge(b_in, 16 * 3)
            pe.transpose(y[:, 0, 0:21], brow[:, :], ident[0:21, 0:21]).then_inc(bT_turned, 1)
            first_layer_l0(b, 1)
            pe.wait_ge(bT_ready, 1)
            l0_block(b, lambda p: first_layer_l0(Block("mixed", 1), p), True, first_hooks)
            with pe.Fori(0, NBM - 1) as r:
                l0_block(Block("mixed", 1, r), lambda p: first_layer_l0(Block("mixed", 2, r), p), True)
            for k, hooks in ((NBM, fifth_hooks), (NBM + 1, sixth_hooks)):
                l0_block(Block("proprio", k), lambda p, k=k: first_layer_l0(Block("proprio", k + 1), p), True, hooks)
            l0_block(Block("proprio", NB - 1), lambda p: first_layer_l1(Block("l1", 0, first=True), p),
                     False, last_hooks)

            def early_hooks(k):
                def hooks(p):
                    if k == 0 and p == 5:
                        route(NB - 2, m[:, 1, :], EARLY)
                        route(NB - 1, m[:, 1, :], EARLY).then_inc(logits1, 1)
                    if k == LATE_TURN and p == 5:
                        turn_gates(RUNS - 1, RUNS, 2)
                return hooks

            for k in range(PEELED):
                l1_block(Block("l1", k, first=k == 0),
                         lambda p, k=k: first_layer_l1(Block("l1", k + 1), p), early_hooks(k))
            with pe.Fori(0, NB - 1 - PEELED) as r:
                l1_block(Block("l1", PEELED, r), lambda p: first_layer_l1(Block("l1", PEELED + 1, r), p))
            l1_block(Block("l1", NB - 1))
            pe.wait_ge(bank_read, NB - 1)
            for k, bank in enumerate((y[:, 1, :], m[:, 0, :])):
                pe.wait_ge(y_used, 2 * NB + k)
                for t in range(2):
                    last = pe.transpose(bank[:, t * P:(t + 1) * P], x2T[:, (2 * k + t) * P:(2 * k + t + 1) * P],
                                        ident[:, :])
                last.then_inc(out_turned, 1)

        @block.vector
        def _(dve):
            steps = [0]

            def link(ins):
                steps[0] += 1
                ins.then_inc(dve_step, 1)
                dve.wait_ge(dve_step, steps[0])

            def tt(out_, a, b_, op):
                return dve.tensor_tensor(out_, a, b_, op)

            def x_copy(columns, number):
                dve.wait_ge(x_turned, number)
                dve.tensor_copy(xT[:, columns], m[:, 0, :]).then_inc(xT_done, 1)

            def split_l0(b, p):
                buf = p % 2
                if p % 2 == 0:
                    dve.wait_ge(hi_act, b.halves + (p // 2 + 1))
                else:
                    dve.wait_ge(h_ready, b.pairs + (p + 1))
                    if not (b.first and p < 2):
                        dve.wait_ge(mm2_done, b.pairs + (p - 1))
                    dve.tensor_copy(hhi[:, buf, :, :], h[:, buf, :, :]).then_inc(hi_dve, 1)
                    dve.wait_ge(hi_dve, b.halves + (p // 2 + 1))
                tt(hlo[:, buf, :, :], h[:, buf, :, :], hhi[:, buf, :, :].bitcast(F32),
                   ALU.subtract).then_inc(split_done, 1)

            def job_out(b, j, columns):
                n_jobs = len(JOBS[b.kind])
                bank = (n_jobs - 1 - j) % 2
                dve.wait_ge(mm2_done, b.pairs + (2 * j + 2))
                if j == 0:
                    if not b.first:
                        dve.wait_ge(x1_ready, b.index * 2)
                    tt(acc[:, :], y[:, bank, :], xT[:, columns], ALU.add).then_inc(y_used, 1)
                    return
                if b.first and j < 3:
                    dve.wait_ge(w_ready, 3)
                    dve.tensor_copy(part_of(b, j), y[:, bank, :]).then_inc(part_ready, 1)
                    return
                dve.wait_ge(wb_ready, 1)
                if j >= 3 and not b.first:
                    dve.wait_ge(adds_done, b.adds + (j - 2))
                if JOBS[b.kind][j] is BOTH:
                    weights = wb[:, 1:3, :].unsqueeze(2).to_broadcast([P, 2, 2, P])
                    shape = dict(a=2, b=2)
                    src = y[:, bank, :].rearrange("p (a b c) -> p a b c", **shape)
                    dst = part[:, j % 2, :].rearrange("p (a b c) -> p a b c", **shape)
                else:
                    e = JOBS[b.kind][j][0][0]
                    weights = wb[:, e, :].unsqueeze(1).to_broadcast([P, TB, P])
                    src = y[:, bank, :].rearrange("p (b c) -> p b c", b=TB)
                    dst = part[:, j % 2, :].rearrange("p (b c) -> p b c", b=TB)
                tt(dst, src, weights, ALU.mult).then_inc(part_ready, 1)

            def close_l0(b, steps=(0, 1)):
                if 0 in steps:
                    dve.wait_ge(adds_done, b.adds + l0_last_adds(b.kind))
                    dve.tensor_copy(xhi[:, b.columns], acc[:, :]).then_inc(x1hi_done, 1)
                    dve.tensor_copy(xT[:, b.columns], acc[:, :]).then_inc(x1_ready, 1)
                if 1 not in steps:
                    return
                dve.wait_ge(x1hi_done, b.index + 1)
                tt(xlo[:, b.columns], acc[:, :], xhi[:, b.columns].bitcast(F32),
                   ALU.subtract).then_inc(x1_ready, 1)

            def l0_block(b, before, next_x, hooks=None):
                n_jobs = len(JOBS[b.kind])
                for p in range(2 * n_jobs):
                    split_l0(b, p)
                    if p == 3 and next_x:
                        x_copy(b.shifted(1), b.index + 2)
                    if before is not None and p == 0:
                        job_out(before, len(JOBS[before.kind]) - 1, before.columns)
                    late = before is not None and before.first
                    if before is not None and p == (3 if late else 1):
                        close_l0(before)
                    if hooks:
                        hooks(p)
                    if p >= 4 and p % 2 == 0 or p == (3 if late else 2):
                        job_out(b, p // 2 - 1, b.columns)

            def cond_prepare():
                dve.wait_ge(c_tanh, 1)
                link(dve.scalar_tensor_tensor(out=csig[:, 1, :], in0=csig[:, 0, :], scalar=1.0, in1=cnat[:, :],
                                              op0=ALU.add, op1=ALU.mult))
                dve.tensor_scalar(silu[:, :], csig[:, 1, :], 0.5, None, ALU.mult).then_inc(silu_ready, 1)

            def positions_sum(k):
                dve.wait_ge(xnat_in[k], 16)
                if k < 2:
                    src = hw(xnat)[:, :, 0:TB, :] if k == 0 else hw(xnat)[:, :, TB:, :]
                    link(dve.tensor_reduce(sums[:, 2 * k:2 * k + 2, :], src.rearrange("p s l d -> p s d l"), AX, ALU.add))
                else:
                    link(dve.tensor_reduce(sums[:, 4, :], xnat[:, 2 * LH:, :].rearrange("p l d -> p d l"), AX, ALU.add))

            def gate_sums():
                link(tt(sums[:, 0:2, :], sums[:, 0:2, :], sums[:, 2:4, :], ALU.add))
                tt(agg[:, 1:3, :], sums[:, 0:2, :], sums[:, 4, :].unsqueeze(1).to_broadcast([P, 2, P]),
                   ALU.add).then_inc(agg_ready, 1)
                dve.wait_ge(agg_ready, 1)
                tt(agg[:, 0, :], agg[:, 1, :], sums[:, 1, :], ALU.add).then_inc(agg_ready, 1)

            def gate_means():
                dve.wait_ge(agg_turned, 1)
                dve.tensor_scalar(aggT[:, 0, :], m[:, 1, 0:P], 1.0 / L, None, ALU.mult).then_inc(aggT_ready, 1)
                dve.tensor_scalar(aggT[:, 1:3, :], m[:, 1, P:3 * P].rearrange("p (a d) -> p a d", a=2),
                                  1.0 / (LH + LP), None, ALU.mult).then_inc(aggT_ready, 1)

            def gate_shift():
                dve.wait_ge(logits0, 1)
                link(dve.scalar_tensor_tensor(out=g0[:, 0, :], in0=rows[:, 0:E0], scalar=1.0, in1=m[:, 1, 408:412],
                                              op0=ALU.add, op1=ALU.mult))
                tt(g0[:, 1, :], g0[:, 0, :], rows[:, E0:2 * E0], ALU.add).then_inc(shifted0, 1)
                dve.wait_ge(shifted0, 1)
                dve.tensor_reduce(g0s[:, 0:1], g0[:, 1, :], AX, ALU.max, negate=True).then_inc(shifted0, 1)

            def find_best(values, found):
                best, scratch = g0s[:, 3:4], g0[:, 4, :]
                link(dve.tensor_reduce(best, values, AX, ALU.max))
                link(dve.scalar_tensor_tensor(out=scratch, in0=values, scalar=best, in1=order[:, E1 - E0:],
                                              op0=ALU.is_equal, op1=ALU.mult))
                link(dve.tensor_reduce(best, scratch, AX, ALU.max))
                link(dve.tensor_scalar(found, scratch, best, None, ALU.is_equal))

            def gate_weights(step):
                if step == 0:
                    dve.wait_ge(exp0, 1)
                    link(dve.reciprocal(g0s[:, 2:3], g0s[:, 1:2]))
                    link(dve.tensor_scalar(g0[:, 3, :], g0[:, 2, :], g0s[:, 2:3], None, ALU.mult))
                    find_best(g0[:, 3, :], g0[:, 5, :])
                    link(dve.scalar_tensor_tensor(out=g0[:, 6, :], in0=g0[:, 5, :], scalar=-BIG, in1=g0[:, 3, :],
                                                  op0=ALU.mult, op1=ALU.add))
                if step == 1:
                    find_best(g0[:, 6, :], g0[:, 7, :])
                    link(tt(g0[:, 4, :], g0[:, 5, :], g0[:, 7, :], ALU.add))
                    link(tt(g0[:, 5, :], g0[:, 4, :], g0[:, 3, :], ALU.mult))
                    link(dve.tensor_reduce(g0s[:, 4:5], g0[:, 5, :], AX, ALU.add))
                    link(dve.tensor_scalar(g0s[:, 5:6], g0s[:, 4:5], 1e-8, None, ALU.add))
                    link(dve.reciprocal(g0s[:, 4:5], g0s[:, 5:6]))
                    dve.tensor_scalar(wbe[:, :], g0[:, 5, :], g0s[:, 4:5], None, ALU.mult).then_inc(wbe_ready, 1)

            def spread_l0():
                dve.wait_ge(w_turned, 1)
                link(dve.tensor_copy(wT[:, :], m[0:E0, 1, 0:P]))
                tt(wdiag[:, :, :], wT[:, :].unsqueeze(1).to_broadcast([E0, E0, P]),
                   ident[0:E0, 0:E0].unsqueeze(2).to_broadcast([E0, E0, P]), ALU.mult).then_inc(wd_ready, 1)
                tt(wmask[:, :, :], wT[:, :].unsqueeze(1).to_broadcast([E0, 3, P]),
                   mask3[:, :].unsqueeze(2).to_broadcast([E0, 3, P]), ALU.mult).then_inc(wd_ready, 1)
                dve.wait_ge(wb_mm, 1)
                dve.tensor_copy(wb[:, :, :], m[:, 1, :].rearrange("p (e b) -> p e b", e=E0)).then_inc(wb_ready, 1)

            def spread_base():
                dve.wait_ge(wb_mm, 2)
                dve.tensor_scalar(base[:, :, :], m[:, 0, 0:3 * P].rearrange("p (k b) -> p k b", k=3),
                                  bT[:, 20:21], None, ALU.add).then_inc(wb_ready, 1)

            def first_hooks(p):
                if p == 1:
                    positions_sum(2)
                    gate_sums()
                    dve.wait_ge(rows_mm, 1)
                    dve.tensor_copy(rows[:, :], m[:, 1, 384:408]).then_inc(rows_ready, 1)
                if p == 2:
                    gate_means()
                if p == 3:
                    gate_shift()
                if p == 4:
                    gate_weights(0)
                if p == 5:
                    gate_weights(1)
                if p == 6:
                    dve.tensor_copy(rsplit[:, 0, :], rw[:, 0, :]).then_inc(r_ready, 1)
                    dve.wait_ge(r_ready, 1)
                    tt(rsplit[:, 1, :], rw[:, 0, :], rsplit[:, 0, :].bitcast(F32), ALU.subtract).then_inc(r_ready, 1)
                if p == 7:
                    spread_l0()

            def logits_l1(t0, t1, number):
                t = t1 - t0
                parts = m[:, 1, 0:t * 2 * E1].rearrange("p (t k e) -> p t k e", k=2, e=E1)
                value, work = g1[:, 0, t0:t1, :], g1[:, 2, t0:t1, :]
                dve.wait_ge(logits1, number)
                link(tt(work, parts[:, :, 0, :], rows[:, 8:16].unsqueeze(1).to_broadcast([P, t, E1]), ALU.add))
                tt(value, work, parts[:, :, 1, :], ALU.add).then_inc(logits1_ready, 1)

            def choose_l1(step, t0, t1, number):
                t = t1 - t0
                value, score, work, chosen, second = (g1[:, k, t0:t1, :] for k in range(5))
                best, denom, inverse, over, half = (g1s[:, k, t0:t1] for k in range(5))

                def wide(v):
                    return v.unsqueeze(2).to_broadcast([P, t, E1])

                def reciprocal(a0, a1):
                    link(dve.reciprocal(g1[:, 1, a0:a1, :], g1[:, 2, a0:a1, :]))

                middle = (t0 + t1) // 2
                if step == 0:
                    dve.wait_ge(exp1, number)
                    link(dve.tensor_scalar(work, score, 1.0, None, ALU.add))
                    reciprocal(t0, middle)
                if step == 1:
                    reciprocal(middle, t1)
                    link(tt(value, score, rows[:, 16:24].unsqueeze(1).to_broadcast([P, t, E1]), ALU.add))
                if step in (2, 5):
                    link(dve.tensor_reduce(best, value, AX, ALU.max))
                    link(tt(work, value, wide(best), ALU.is_equal))
                if step in (3, 6):
                    link(tt(work, work, order[:, :].unsqueeze(1).to_broadcast([P, t, E1]), ALU.mult))
                    link(dve.tensor_reduce(best, work, AX, ALU.max))
                if step in (4, 7):
                    link(tt(chosen if step == 4 else second, work, wide(best), ALU.is_equal))
                if step == 4:
                    link(dve.scalar_tensor_tensor(out=value, in0=chosen, scalar=-BIG, in1=value,
                                                  op0=ALU.mult, op1=ALU.add))
                if step == 7:
                    link(tt(chosen, chosen, second, ALU.add))
                if step == 8:
                    link(tt(work, chosen, score, ALU.mult))
                    link(dve.tensor_reduce(denom, work, AX, ALU.add))
                    link(dve.tensor_scalar(half, denom, 1e-9, None, ALU.add))
                if step == 9:
                    link(dve.tensor_scalar(over, denom, 1e-9, None, ALU.is_gt))
                    link(dve.reciprocal(inverse, half))
                    link(tt(inverse, inverse, over, ALU.mult))
                    dve.tensor_scalar(half, over, -0.5, 0.5, ALU.mult, ALU.add).then_inc(gates_scaled, 1)

            def sixth_hooks(p):
                if p == 3:
                    logits_l1(0, EARLY, 1)
                if p >= 5:
                    choose_l1(p - 5, 0, EARLY, 1)

            def last_hooks(p):
                step = {0: 5, 2: 6, 3: 7, 4: 8, 5: 9}.get(p)
                if step:
                    choose_l1(step, 0, EARLY, 1)

            def gate_routed(b, p, between=None):
                buf, own = p % 2, h1[p % 3]
                if p == 2:
                    dve.wait_ge(wide_in[b.parity], b.of_parity * 16 + 16)
                dve.wait_ge(h_ready, b.pairs + (p + 1))
                for j in range(2):
                    e = 2 * (p - 2) + j
                    tt(own[:, j, :], own[:, j, :], wide_gates[b.parity][:, e * BW:(e + 1) * BW],
                       ALU.mult).then_inc(gated, 1)
                if between:
                    between(p)
                dve.wait_ge(ghi_done, b.chunks + (2 * (p - 2) + 1))
                tt(hlo[:, buf, 0, :], own[:, 0, :], hhi[:, buf, 0, :].bitcast(F32),
                   ALU.subtract).then_inc(split_done, 1)

            def gate_shared(b):
                for p in range(C1):
                    dve.wait_ge(h_ready, b.pairs + (p + 1))
                    dve.wait_ge(z_ready, b.pairs * 2 + (2 * p + 2))
                    dve.scalar_tensor_tensor(out=h[:, p, 1, :], in0=h[:, p, 0, :], scalar=1.0, in1=z[:, 2 * p, :],
                                             op0=ALU.add, op1=ALU.mult).then_inc(half_gated, 1)
                    dve.wait_ge(half_gated, b.shared + (p + 1))
                    dve.scalar_tensor_tensor(out=h[:, p, 0, :], in0=h[:, p, 1, :], scalar=0.5,
                                             in1=z[:, 2 * p + 1, :], op0=ALU.mult, op1=ALU.mult).then_inc(swiglu, 1)
                if not b.first:
                    close_l1(b.pairs, b.index, b.shifted(-1))
                for p in range(C1):
                    dve.wait_ge(shared_hi, b.shared + (p + 1))
                    tt(hlo[:, p, 0, :], h[:, p, 0, :], hhi[:, p, 0, :].bitcast(F32),
                       ALU.subtract).then_inc(split_done, 1)

            def close_l1(pairs, number, columns, halves=1):
                dve.wait_ge(mm2_done, pairs)
                if not (isinstance(number, int) and number == 1):
                    dve.wait_ge(bank_read, number - 1)
                if halves == 1:
                    dve.scalar_tensor_tensor(out=x2T, in0=y[:, 0, :], scalar=1.0 / 3.0, in1=xT[:, columns],
                                             op0=ALU.mult, op1=ALU.add).then_inc(y_used, 1)
                    return
                for k in (0, HW):
                    dve.scalar_tensor_tensor(out=x2T[:, k:k + HW], in0=y[:, 0, k:k + HW], scalar=1.0 / 3.0,
                                             in1=xT[:, columns.start + k:columns.start + k + HW],
                                             op0=ALU.mult, op1=ALU.add).then_inc(y_used, 1)

            def l1_block(b, between=None):
                gate_shared(b)
                if between:
                    between(0)
                for p in range(C1, L1_PAIRS):
                    gate_routed(b, p, between)

            last_l0 = Block("proprio", NB - 1)

            def first_l1(p):
                if p == 0:
                    job_out(last_l0, len(JOBS["proprio"]) - 1, last_l0.columns)
                if p == 3:
                    close_l0(last_l0, steps=(0,))
                if p == 4:
                    close_l0(last_l0, steps=(1,))

            def second_l1(p):
                if p == 0:
                    logits_l1(EARLY, L, 2)

            def choose_last(p, of):
                for step in {(2, 2): (0,), (2, 3): (1,), (2, 4): (2, 3), (2, 5): (4, 5),
                             (3, 2): (6, 7), (3, 3): (8, 9)}.get((of, p), ()):
                    choose_l1(step, EARLY, L, 2)

            cond_prepare()
            x_copy(slice(0, BW), 1)
            dve.wait_ge(c_turned, 1)
            dve.tensor_copy(cT[:, :, :], m[:, 1, 0:2 * P].rearrange("p (a d) -> p a d", a=2)).then_inc(c_ready, 1)
            dve.wait_ge(xT_done, 1)
            dve.wait_ge(xhi_done, 1)
            tt(xlo[:, 0:BW], xT[:, 0:BW], xhi[:, 0:BW].bitcast(F32), ALU.subtract).then_inc(x_ready, 1)
            positions_sum(0)
            dve.wait_ge(bT_turned, 1)
            dve.tensor_copy(bT[:, :], y[:, 0, 0:21]).then_inc(bT_ready, 1)
            positions_sum(1)
            l0_block(Block("mixed", 0, first=True), None, True, first_hooks)
            l0_block(Block("mixed", 1), Block("mixed", 0, first=True), True,
                     lambda p: spread_base() if p == 0 else None)
            with dve.Fori(0, NBM - 2) as r:
                l0_block(Block("mixed", 2, r), Block("mixed", 1, r), True)
            l0_block(Block("proprio", NBM), Block("mixed", NBM - 1), True)
            l0_block(Block("proprio", NBM + 1), Block("proprio", NBM), True, sixth_hooks)
            l0_block(Block("proprio", NB - 1), Block("proprio", NB - 2), False, last_hooks)
            l1_block(Block("l1", 0, first=True), first_l1)
            l1_block(Block("l1", 1), second_l1)
            l1_block(Block("l1", 2), lambda p: choose_last(p, 2))
            l1_block(Block("l1", 3), lambda p: choose_last(p, 3))
            with dve.Fori(0, (NB - 4) // 2) as r:
                l1_block(Block("l1", 4, r * 2, of_parity=r + 2))
                l1_block(Block("l1", 5, r * 2, of_parity=r + 2))
            close_l1(L0_PAIRS + L1_PAIRS * NB, NB, slice((NB - 1) * BW, NB * BW), halves=2)


_L0 = ["gate_w", "gate_b", "time_w", "time_b", "ew1", "eb1", "ew2", "eb2", "sw1", "sb1", "sw2", "sb2"]
_L1 = ["router_W", "router_bias", "w1", "w3", "w2", "W1e", "W2e"]
_INS = ["x", "cond_1024"] + ["L0_cond_" + n for n in _L0] + ["L1_cond_" + n for n in _L1]
_OUTS = [((P, L, P), "float32")]


def kernel(**inputs):
    import numpy as _np
    import concourse.bacc as _bacc
    from concourse import mybir as _mybir
    from concourse.bass_utils import run_bass_kernel_spmd as _run

    nc = _bacc.Bacc("TRN2", target_bir_lowering=False, num_devices=1)
    arrays, args = {}, []
    for name in _INS:
        a = _np.ascontiguousarray(inputs[name])
        arrays[f"in_{name}_dram"] = a
        args.append(nc.dram_tensor(f"in_{name}_dram", a.shape, _mybir.dt.from_np(a.dtype), kind="ExternalInput").ap())
    for i, (shape, dtype) in enumerate(_OUTS):
        dt = _mybir.dt.from_np(_np.dtype(dtype))
        args.append(nc.dram_tensor(f"out_{i}_dram", shape, dt, kind="ExternalOutput").ap())
    build(nc, *args)
    r = _run(nc, [arrays], core_ids=[0])
    return r.results[0]["out_0_dram"]
```
